# Optimizing a Trainium2 kernel written in Bass

```python
import numpy as np
import jax
import jax.numpy as jnp

def _softmax(x, axis=-1):
    return jax.nn.softmax(x, axis=axis)

def _gelu(x):
    return jax.nn.gelu(x, approximate=True)

def _silu(x):
    return jax.nn.silu(x)

def _sigmoid(x):
    return jax.nn.sigmoid(x)

def _layernorm(x, axis=-1, eps=1e-05):
    m = jnp.mean(x, axis=axis, keepdims=True)
    v = jnp.var(x, axis=axis, keepdims=True)
    return (x - m) / jnp.sqrt(v + eps)

def _scatter_add(tgt, idx, src, axis=0):
    return tgt.at[idx].add(src)

def _segment_sum(src, seg, n):
    return jax.ops.segment_sum(src, seg, n)
kernel_name = 'mk_adj_ffn_d1_adj_r2_e1c610'

def setup_inputs(seed: int=0):
    np.random.seed(seed)
    _w = jnp.asarray

    def _rec_inputs():
        import jax
        import jax.numpy as jnp
        _gk = jax.random.key(seed)
        x = -0.0002928 + 1 * jax.random.normal(jax.random.fold_in(_gk, 1), (3327, 256), jnp.float32)
        _a = jax.random.bernoulli(jax.random.fold_in(_gk, 2), 0.00480914, (3327, 3327))
        adj = _a
        return (x, adj)
    x, adj = _rec_inputs()

    def _L0_gnn_setup():
        import jax, jax.numpy as jnp
        import numpy as np
        N = 4096
        D = 256
        NEG = -1e+30
        key = jax.random.key(seed)
        ks = jax.random.split(key, 5)
        neuron_states = jax.random.normal(ks[0], (N, D), dtype=jnp.float32)
        adjacency = jax.random.bernoulli(ks[1], 0.05, (N, N))
        Wq = jax.random.normal(ks[2], (D, D), dtype=jnp.float32) / np.sqrt(D)
        Wk = jax.random.normal(ks[3], (D, D), dtype=jnp.float32) / np.sqrt(D)
        Wv = jax.random.normal(ks[4], (D, D), dtype=jnp.float32) / np.sqrt(D)
        return {'neuron_states': neuron_states, 'adjacency': adjacency, 'Wq': Wq, 'Wk': Wk, 'Wv': Wv}
    _L0_gnn_all = _L0_gnn_setup()
    _L0_gnn_in = {k: v for k, v in _L0_gnn_all.items() if k in ('Wq', 'Wk', 'Wv')}
    del _L0_gnn_all

    def _L0_ffn_setup():
        import jax, jax.numpy as jnp
        import numpy as np
        E = 64
        K = 2
        CAP = 256
        H = 256
        FFN = 1024
        B, S = (8, 2048)
        key = jax.random.key(seed)
        ks = jax.random.split(key, 6)
        hidden_states = jax.random.normal(ks[0], (B, S, H), dtype=jnp.float32)
        router_w = jax.random.normal(ks[1], (E, H), dtype=jnp.float32) * (0.01 / np.sqrt(H))
        w1 = jax.random.normal(ks[2], (FFN, H), dtype=jnp.float32) * (1.0 / np.sqrt(H))
        b1 = jnp.zeros((FFN,), dtype=jnp.float32)
        w2 = jax.random.normal(ks[3], (H, FFN), dtype=jnp.float32) * (1.0 / np.sqrt(FFN))
        b2 = jnp.zeros((H,), dtype=jnp.float32)
        return {'hidden_states': hidden_states, 'router_w': router_w, 'w1': w1, 'b1': b1, 'w2': w2, 'b2': b2}
    _L0_ffn_all = _L0_ffn_setup()
    _L0_ffn_in = {k: v for k, v in _L0_ffn_all.items() if k in ('router_w', 'w1', 'b1', 'w2', 'b2')}
    del _L0_ffn_all
    return {'x': x, 'adj': adj, 'L0_gnn_Wq': _L0_gnn_in['Wq'], 'L0_gnn_Wk': _L0_gnn_in['Wk'], 'L0_gnn_Wv': _L0_gnn_in['Wv'], 'L0_ffn_router_w': _L0_ffn_in['router_w'], 'L0_ffn_w1': _L0_ffn_in['w1'], 'L0_ffn_b1': _L0_ffn_in['b1'], 'L0_ffn_w2': _L0_ffn_in['w2'], 'L0_ffn_b2': _L0_ffn_in['b2']}

def reference(x, adj, L0_gnn_Wq, L0_gnn_Wk, L0_gnn_Wv, L0_ffn_router_w, L0_ffn_w1, L0_ffn_b1, L0_ffn_w2, L0_ffn_b2):
    import jax
    import jax.numpy as jnp

    def _L0_gnn_ref(neuron_states, adjacency, Wq, Wk, Wv):
        import jax, jax.numpy as jnp
        import numpy as np
        N = 4096
        D = 256
        NEG = -1e+30
        q = neuron_states @ Wq.T
        k = neuron_states @ Wk.T
        v = neuron_states @ Wv.T
        mask = adjacency.T
        scores = jnp.where(mask, q @ k.T, NEG)
        attn = jax.nn.softmax(scores, axis=1)
        attn = jnp.where(mask, attn, 0.0)
        return attn @ v

    def _L0_ffn_ref(hidden_states, router_w, w1, b1, w2, b2):
        import jax, jax.numpy as jnp
        import numpy as np
        E = 64
        K = 2
        CAP = 256
        H = 256
        FFN = 1024
        B, S = (8, 2048)
        orig_shape = hidden_states.shape
        x = hidden_states.reshape(-1, orig_shape[-1])
        T = x.shape[0]
        N = T * K
        logits = jnp.einsum('th,eh->te', x, router_w)
        probs_full = jax.nn.softmax(logits, axis=-1)
        probs, idx = jax.lax.top_k(probs_full, K)
        flat_e = idx.reshape(-1)
        flat_p = probs.reshape(-1)
        order = jnp.argsort(flat_e, stable=True)
        sorted_e = flat_e[order]
        counts = jnp.zeros((E,), jnp.int32).at[flat_e].add(1)
        offsets = jnp.concatenate([jnp.zeros((1,), jnp.int32), jnp.cumsum(counts)[:-1]])
        pos = jnp.arange(N, dtype=jnp.int32) - offsets[sorted_e]
        keep = pos < CAP
        slot = sorted_e * CAP + jnp.minimum(pos, CAP - 1)
        dest = jnp.where(keep, slot, E * CAP)
        tok = order // K
        buf = jnp.zeros((E * CAP + 1, x.shape[-1]), x.dtype).at[dest].set(x[tok])
        buf = buf[:-1]
        h = jax.nn.gelu(jnp.einsum('nh,fh->nf', buf, w1) + b1, approximate=False)
        y = jnp.einsum('nf,hf->nh', h, w2) + b2
        gate = jnp.where(keep, flat_p[order], 0.0)
        contrib = y[jnp.minimum(slot, E * CAP - 1)] * gate[:, None]
        out = jnp.zeros_like(x).at[tok].add(contrib)
        return out.reshape(orig_shape)
    x = x + _L0_gnn_ref(_layernorm(x, axis=-1), adj, L0_gnn_Wq, L0_gnn_Wk, L0_gnn_Wv)
    x = x + _L0_ffn_ref(_layernorm(x, axis=-1)[None], L0_ffn_router_w, L0_ffn_w1, L0_ffn_b1, L0_ffn_w2, L0_ffn_b2)[0]
    return x

_drawn_inputs = setup_inputs


def setup_inputs(seed=0):
    import zlib

    import numpy as np

    out = dict(_drawn_inputs(seed))
    spreads = {'L0_ffn_b1': (0.0, 0.8), 'L0_ffn_b2': (0.0, 2.0)}
    factors = {'L0_ffn_router_w': 26.008, 'L0_ffn_w1': 4.132, 'L0_ffn_w2': 3.698}
    for name, (base, spread) in spreads.items():
        noise = np.random.default_rng([zlib.crc32(name.encode()), seed]).standard_normal(out[name].shape)
        drawn = base * np.exp(spread * noise) if base else spread * noise
        out[name] = jnp.asarray(drawn.astype(out[name].dtype))
    for name, factor in factors.items():
        out[name] = (out[name] * factor).astype(out[name].dtype)
    return out
```

```python
from contextlib import ExitStack

import concourse.bass as bass
from concourse import mybir

ACT = mybir.ActivationFunctionType
ALU = mybir.AluOpType
AX = mybir.AxisListType
F32 = mybir.dt.float32
F32R = mybir.dt.float32r
BF16 = mybir.dt.bfloat16
FP8 = mybir.dt.float8e4
U8 = mybir.dt.uint8
U32 = mybir.dt.uint32

P = 128
EPS = 1e-5
CAPACITY = 256
NO_EDGE_BYTE_SHIFT = 6
NO_EDGE = -1e30
BIG = 3e38


def ds(start, size):
    return bass.ds(start, size)


def at_least(engine, semaphore, value):
    if not isinstance(value, int) or value > 0:
        engine.wait_ge(semaphore, value)


def build(nc, x, adj, Wq, Wk, Wv, router_w, w1, b1, w2, b2, out):
    N, D = x.shape
    E = router_w.shape[0]
    F = w1.shape[0]
    TILES = (N + P - 1) // P
    LAST = N - (TILES - 1) * P
    BLOCKS = TILES // 2
    KEYS = TILES * P
    KC = D // P
    B = 2 * P
    CHUNK = 512
    CH = (KEYS + CHUNK - 1) // CHUNK
    FT = F // P
    FP = FT // 2
    VW = D + 2
    HEAD = 2 * CHUNK
    assert TILES == 2 * BLOCKS and BLOCKS > 3 and D == 256 and F % B == 0

    def width(g):
        return min(CHUNK, KEYS - g * CHUNK)

    with ExitStack() as ctx:
        def sb(name, shape, dt):
            return ctx.enter_context(nc.sbuf_tensor(name, shape, dt))

        def sem(name):
            return ctx.enter_context(nc.semaphore(name))

        tokens = sb("tokens", [P, TILES * D], F32)
        xnT_hi = sb("xnT_hi", [P, KC, KEYS], F32R)
        xnT_lo = sb("xnT_lo", [P, KC, KEYS], F32R)
        v_hi = sb("v_hi", [P, TILES * VW], F32R)
        v_lo = sb("v_lo", [P, TILES * VW], F32R)
        probs = sb("probs", [P, 2, KEYS], F32)
        probsT_hi = sb("probsT_hi", [P, 2, CHUNK], F32R)
        probsT_lo = sb("probsT_lo", [P, 2, CHUNK], F32R)
        bytes_sb = sb("bytes_sb", [P, 2, TILES, B], U8)
        qT_hi = sb("qT_hi", [P, KC, B], F32R)
        qT_lo = sb("qT_lo", [P, KC, B], F32R)
        a_hi = sb("a_hi", [P, KC, D], F32R)
        a_lo = sb("a_lo", [P, KC, D], F32R)
        xhat = sb("xhat", [P, 2, D], F32)
        rT_hi = sb("rT_hi", [P, KC, P], F32R)
        rT_lo = sb("rT_lo", [P, KC, P], F32R)
        rwT_hi = sb("rwT_hi", [P, KC, E], F32R)
        rwT_lo = sb("rwT_lo", [P, KC, E], F32R)
        ident = sb("ident", [P, P], F32)
        no_edge = sb("no_edge", [P, P], BF16)
        before = sb("before", [P, P], BF16)
        ones = sb("ones", [P, P], BF16)
        rev = sb("rev", [P, E], F32)
        minus_half = sb("minus_half", [P, TILES], F32)
        stats = sb("stats", [P, TILES * 6], F32)
        mean1 = sb("mean1", [P, TILES], F32)
        rstd1 = sb("rstd1", [P, TILES], F32)
        mean2 = sb("mean2", [P, TILES], F32)
        rstd2 = sb("rstd2", [P, TILES], F32)
        gates = sb("gates", [P, TILES], F32)
        tmp1 = sb("tmp1", [P, TILES], F32)
        tmp2 = sb("tmp2", [P, TILES], F32)
        chunk_max = sb("chunk_max", [P, 2, CH], F32)
        row_max = sb("row_max", [P, 2], F32)
        minus_max = sb("minus_max", [P, 2], F32)
        has_edge = sb("has_edge", [P, 2], F32)
        inv_sum = sb("inv_sum", [P, 2], F32)
        row_scale = sb("row_scale", [P, 2], F32)
        stats2 = sb("stats2", [P, 6], F32)
        meanvar2 = sb("meanvar2", [P, 2], F32)
        var_eps = sb("var_eps", [P, 1], F32)
        best = sb("best", [P, 8], F32)
        cand = sb("cand", [P, E], F32)
        first = sb("first", [P, E], F32)
        rest = sb("rest", [P, E], F32)
        picked = sb("picked", [P, E], BF16)
        logits_sb = sb("logits_sb", [P, E], F32)
        router_exp = sb("router_exp", [P, E], F32)
        router_sum = sb("router_sum", [P, 1], F32)
        rank = sb("rank", [P, E], F32)
        kept = sb("kept", [P, E], F32)
        queue = sb("queue", [P, E], F32)
        b1_sb = sb("b1_sb", [P, FT], F32)
        b2_sb = sb("b2_sb", [P, D], F32)

        raw = bytes_sb[:, 0]
        missing = bytes_sb[:, 1]
        wnat = probs[:, 0, 0:3 * KC * D].rearrange("p (w k d) -> p w k d", w=3, k=KC)
        rwnat = probs[0:E, 1, 0:D]
        wvT_hi = probsT_hi[:, 0, :].rearrange("p (k d) -> p k d", k=KC)
        wvT_lo = probsT_lo[:, 0, :].rearrange("p (k d) -> p k d", k=KC)
        w1nat = probs[:, 0, 0:FT * D].rearrange("p (f d) -> p f d", f=FT)
        w2nat = bytes_sb[:].rearrange("p a t b -> p (a t b)")[:, 0:4 * KC * F].bitcast(F32) \
            .rearrange("p (k f) -> p k f", k=KC)
        w1T = [s[:, 0, 0:KC * F].rearrange("p (k f) -> p k f", k=KC) for s in (xnT_hi, xnT_lo)]
        w2T = [s[:, 1, 0:FT * D].rearrange("p (f d) -> p f d", f=FT) for s in (xnT_hi, xnT_lo)]
        hT = probs[:, 1, 0:FT * B].rearrange("p (f b) -> p f b", f=FT)
        hT_hi = v_hi[:, 0:FT * B].rearrange("p (f b) -> p f b", f=FT)
        hT_lo = v_lo[:, 0:FT * B].rearrange("p (f b) -> p f b", f=FT)
        y_sb = probs[:, 0, 0:2 * D].rearrange("p (t d) -> p t d", t=2)

        def bank(name):
            return ctx.enter_context(nc.psum_tensor(name, [P, CHUNK], F32))

        score_ps = [bank(f"score_ps{i}") for i in range(2)]
        turn_ps = [bank(f"turn_ps{i}") for i in range(2)]
        attn_ps = [bank(f"attn_ps{i}") for i in range(2)]
        q_ps = bank("q_ps")
        route_ps = bank("route_ps")
        qT_ps = q_ps[:].rearrange("p (k b) -> p k b", k=KC)
        rT_ps = route_ps[:, 0:KC * P].rearrange("p (k t) -> p k t", k=KC)
        logits_ps = route_ps[:, 256:256 + E]
        rank_ps = route_ps[:, 320:320 + E]
        total_ps = route_ps[:, 384:384 + E]
        hidden_ps = [*score_ps, *turn_ps]
        y_ps = attn_ps

        weights_in = sem("weights_in")
        biases_in = sem("biases_in")
        x_in = [sem(f"x_in{i}") for i in range(2)]
        adj_in = sem("adj_in")
        consts_made = sem("consts_made")
        zeroed = sem("zeroed")
        v_columns_made = sem("v_columns_made")
        pads_made = sem("pads_made")
        a_ready = sem("a_ready")
        a_hi_out = sem("a_hi_out")
        a_split = sem("a_split")
        stats_made = sem("stats_made")
        ln_seq = sem("ln_seq")
        var1_ready = sem("var1_ready")
        rstd1_ready = sem("rstd1_ready")
        xn_ready = sem("xn_ready")
        xn_turned = sem("xn_turned")
        stage_hi = sem("stage_hi")
        stage_split = sem("stage_split")
        stage_kept = sem("stage_kept")
        v_ready = sem("v_ready")
        v_hi_out = sem("v_hi_out")
        v_split = sem("v_split")
        q_ready = sem("q_ready")
        q_hi_out = sem("q_hi_out")
        q_split = sem("q_split")
        mask_ready = sem("mask_ready")
        scores_ready = sem("scores_ready")
        scores_taken = sem("scores_taken")
        max_seq = sem("max_seq")
        minus_max_ready = sem("minus_max_ready")
        exp_done = sem("exp_done")
        probs_turned = sem("probs_turned")
        probs_hi_out = sem("probs_hi_out")
        probs_split = sem("probs_split")
        values_done = sem("values_done")
        attn_taken = sem("attn_taken")
        finish_seq = sem("finish_seq")
        var2_ready = sem("var2_ready")
        rstd2_ready = sem("rstd2_ready")
        xhat_ready = sem("xhat_ready")
        xhat_turned = sem("xhat_turned")
        router_hi_out = sem("router_hi_out")
        router_split = sem("router_split")
        logits_ready = sem("logits_ready")
        route_seq = sem("route_seq")
        best_ready = sem("best_ready")
        router_exp_done = sem("router_exp_done")
        picks_ready = sem("picks_ready")
        ranks_ready = sem("ranks_ready")
        gate_seq = sem("gate_seq")
        gates_ready = sem("gates_ready")
        w1_in = sem("w1_in")
        w2_in = sem("w2_in")
        w_turned = sem("w_turned")
        w_hi_out = sem("w_hi_out")
        w_split = sem("w_split")
        fx_ready = sem("fx_ready")
        fx_turned = sem("fx_turned")
        fx_hi_out = sem("fx_hi_out")
        fx_split = sem("fx_split")
        hidden_ready = sem("hidden_ready")
        gelu_done = sem("gelu_done")
        hidden_hi_out = sem("hidden_hi_out")
        hidden_split = sem("hidden_split")
        hidden_used = sem("hidden_used")
        y_taken = sem("y_taken")
        out_ready = sem("out_ready")
        stored = sem("stored")
        waited_apart = sem("waited_apart")

        FINISH_STEPS, ROUTE_STEPS, GATE_STEPS = 5, 8, 4
        block = ctx.enter_context(nc.Block())

        def wait_apart(engine, semaphore, value):
            at_least(engine, semaphore, value)
            engine.sem_inc(waited_apart, 1)

        def tile_of(m):
            return ds(m * D, D)

        def w_half(i, part):
            if i < FP:
                return w1T[part][:, i // 2, (i % 2) * CHUNK:(i % 2 + 1) * CHUNK]
            return w2T[part][:, 2 * (i - FP):2 * (i - FP) + 2].rearrange("p f d -> p (f d)")

        @block.sync
        def _(sp):
            sp.wait_ge(pads_made, 2)
            xt = tokens[:].rearrange("p (t d) -> p t d", t=TILES)
            half = 12
            sp.dma_start(xt[:, 0:half], x[0:half * P].rearrange("(t p) d -> p t d", p=P)).then_inc(x_in[0], 16)
            sp.dma_start(xt[:, half:TILES - 1], x[half * P:(TILES - 1) * P].rearrange("(t p) d -> p t d", p=P)) \
                .then_inc(x_in[1], 16)
            sp.dma_start(xt[0:LAST, TILES - 1], x[(TILES - 1) * P:N]).then_inc(x_in[1], 16)

            def load_adj(b, cols):
                wait_apart(sp, mask_ready, 2 * b)
                sp.dma_start(raw[:, 0:TILES - 1, 0:cols],
                             adj[0:(TILES - 1) * P, ds(b * B, cols)].rearrange("(t p) c -> p t c", p=P)) \
                    .then_inc(adj_in, 16)
                sp.dma_start(raw[0:LAST, TILES - 1, 0:cols], adj[(TILES - 1) * P:N, ds(b * B, cols)]) \
                    .then_inc(adj_in, 16)

            load_adj(0, B)
            with sp.Fori(1, BLOCKS - 1) as b:
                load_adj(b, B)
            load_adj(BLOCKS - 1, N - (BLOCKS - 1) * B)

            sp.wait_ge(probs_turned, CH * (TILES - 1))
            sp.dma_start(w1nat, w1.rearrange("(f p) d -> p f d", p=P)).then_inc(w1_in, 16)
            sp.wait_ge(scores_ready, CH * TILES)
            sp.dma_start(w2nat, w2.rearrange("(k p) f -> p k f", p=P)).then_inc(w2_in, 16)

            def store(b):
                wait_apart(sp, out_ready, 2 * b + 2)
                sp.dma_start(out[ds(b * B, B)].rearrange("(t p) d -> p t d", p=P),
                             tokens[:, ds(b * 2 * D, 2 * D)].rearrange("p (t d) -> p t d", t=2)) \
                    .then_inc(stored, 16)

            with sp.Fori(0, BLOCKS - 1) as b:
                store(b)
            sp.wait_ge(out_ready, TILES)
            sp.dma_start(out[(TILES - 2) * P:(TILES - 1) * P], xt[:, TILES - 2]).then_inc(stored, 16)
            sp.dma_start(out[(TILES - 1) * P:N], xt[0:LAST, TILES - 1]).then_inc(stored, 16)
            sp.wait_ge(stored, 16 * (BLOCKS + 1))

        @block.gpsimd
        def _(pool):
            g = nc.gpsimd
            g.memset(ident[:], 0.0).then_inc(zeroed, 1)
            g.memset(no_edge[:], 0.0).then_inc(zeroed, 1)
            g.memset(before[:], 0.0).then_inc(zeroed, 1)
            g.memset(ones[:], 1.0).then_inc(consts_made, 1)
            g.memset(minus_half[:], -0.5).then_inc(consts_made, 1)
            pool.wait_ge(zeroed, 3)
            g.affine_select(out=ident[:], in_=ident[:], compare_op=ALU.not_equal, fill=1.0, base=0,
                            pattern=[[-1, P]], channel_multiplier=1).then_inc(consts_made, 1)
            g.affine_select(out=no_edge[:], in_=no_edge[:], compare_op=ALU.not_equal, fill=NO_EDGE / 2, base=0,
                            pattern=[[-1, P]], channel_multiplier=1).then_inc(consts_made, 1)
            g.affine_select(out=before[:], in_=before[:], compare_op=ALU.is_ge, fill=1.0, base=0,
                            pattern=[[-1, P]], channel_multiplier=1).then_inc(consts_made, 1)
            g.iota(rev[:], pattern=[[-1, E]], base=E, channel_multiplier=0,
                   allow_small_or_imprecise_dtypes=True).then_inc(consts_made, 1)

            pool.wait_ge(consts_made, 6)
            pool.wait_ge(var1_ready, 1)
            g.tensor_tensor(rstd1[:], rstd1[:], minus_half[:], ALU.pow).then_inc(rstd1_ready, 1)

            with pool.Fori(0, BLOCKS) as b:
                for t in range(2):
                    m = 2 * b + t
                    pool.wait_ge(stage_split, m + 1)
                    g.tensor_copy(xnT_hi[:, :, ds(m * P, P)], qT_hi[:, :, t * P:(t + 1) * P])
                    g.tensor_copy(xnT_lo[:, :, ds(m * P, P)], qT_lo[:, :, t * P:(t + 1) * P]) \
                        .then_inc(stage_kept, 1)

            with pool.Fori(0, TILES) as m:
                pool.wait_ge(var2_ready, m + 1)
                g.tensor_tensor(rstd2[:, ds(m, 1)], var_eps[:], minus_half[:, 0:1], ALU.pow) \
                    .then_inc(rstd2_ready, 1)

        @block.tensor
        def _(pe):
            def split_product(out_ps, lhs, rhs, start, stop):
                pe.matmul(out_ps, lhs[0], rhs[0], start=start, stop=False)
                pe.matmul(out_ps, lhs[0], rhs[1], start=False, stop=False)
                return pe.matmul(out_ps, lhs[1], rhs[0], start=False, stop=stop)

            pe.wait_ge(weights_in, 16 * 4)
            pe.wait_ge(consts_made, 6)
            for m in range(KC):
                for k in range(KC):
                    mm = pe.matmul(qT_ps[:, m], wnat[:, 0, k, m * P:(m + 1) * P], wnat[:, 1, k],
                                   start=(k == 0), stop=(k == KC - 1))
            mm.then_inc(a_ready, 1)
            for k in range(KC):
                for o in range(KC):
                    mm = pe.transpose(attn_ps[0][:, k * D + o * P:k * D + (o + 1) * P],
                                      wnat[:, 2, o, k * P:(k + 1) * P], ident[:])
            mm.then_inc(a_ready, 1)
            for k in range(KC):
                mm = pe.transpose(route_ps[:, k * E:(k + 1) * E], rwnat[:, k * P:(k + 1) * P], ident[0:E, 0:E])
            mm.then_inc(a_ready, 1)

            def prep_turn(m, t):
                pe.wait_ge(xn_ready, m + 1)
                at_least(pe, stage_split, m - 1)
                for k in range(KC):
                    mm = pe.transpose(turn_ps[t][:, k * P:(k + 1) * P], xhat[:, t, k * P:(k + 1) * P], ident[:])
                mm.then_inc(xn_turned, 1)

            def prep_v(m, t):
                pe.wait_ge(stage_split, m + 1)
                at_least(pe, v_split, m - 1)
                for k in range(KC):
                    cols = slice(t * P, (t + 1) * P)
                    mm = split_product(score_ps[t][:, 0:D], (qT_hi[:, k, cols], qT_lo[:, k, cols]),
                                       (wvT_hi[:, k], wvT_lo[:, k]), k == 0, k == KC - 1)
                mm.then_inc(v_ready, 1)

            prep_turn(0, 0)
            pe.wait_ge(a_split, 3)
            prep_turn(1, 1)
            prep_v(0, 0)
            with pe.Fori(1, BLOCKS) as b:
                prep_turn(2 * b, 0)
                prep_v(2 * b - 1, 1)
                prep_turn(2 * b + 1, 1)
                prep_v(2 * b, 0)
            prep_v(TILES - 1, 1)

            def queries(b):
                at_least(pe, q_split, 2 * b)
                for m in range(KC):
                    for k in range(KC):
                        cols = ds(b * B, B)
                        mm = split_product(qT_ps[:, m], (a_hi[:, k, m * P:(m + 1) * P], a_lo[:, k, m * P:(m + 1) * P]),
                                           (xnT_hi[:, k, cols], xnT_lo[:, k, cols]), k == 0, k == KC - 1)
                mm.then_inc(q_ready, 1)

            def scores(n, t, g):
                if g == 0:
                    pe.wait_ge(q_split, n + 1)
                    pe.wait_ge(mask_ready, n + 1)
                at_least(pe, scores_taken, CH * n + g - 1)
                ps = score_ps[(CH * t + g) % 2]
                w = width(g)
                for k in range(KC):
                    q = (qT_hi[:, k, t * P:(t + 1) * P], qT_lo[:, k, t * P:(t + 1) * P])
                    keys = slice(g * CHUNK, g * CHUNK + w)
                    split_product(ps[:, 0:w], q, (xnT_hi[:, k, keys], xnT_lo[:, k, keys]), k == 0, False)
                for j in range(w // P):
                    mm = pe.matmul(ps[:, j * P:(j + 1) * P],
                                   missing[:, g * (CHUNK // P) + j, t * P:(t + 1) * P].bitcast(FP8),
                                   no_edge[:], start=False, stop=(j == w // P - 1))
                mm.then_inc(scores_ready, 1)

            def turn_probs(m, t, g):
                if g in (0, HEAD // CHUNK):
                    pe.wait_ge(exp_done, 2 * m + 1 + (g > 0))
                at_least(pe, probs_split, CH * m + g - 1)
                ps = turn_ps[(CH * t + g) % 2]
                for j in range(width(g) // P):
                    at = g * CHUNK + j * P
                    mm = pe.transpose(ps[:, j * P:(j + 1) * P], probs[:, t, at:at + P], ident[:])
                mm.then_inc(probs_turned, 1)

            def values(m, t, g):
                pe.wait_ge(probs_split, CH * m + g + 1)
                if g == 0:
                    at_least(pe, attn_taken, m - 1)
                s = (CH * t + g) % 2
                last = width(g) // P - 1
                for j in range(last + 1):
                    key_tile = g * (CHUNK // P) + j
                    hi, lo = probsT_hi[:, s, j * P:(j + 1) * P], probsT_lo[:, s, j * P:(j + 1) * P]
                    v = v_hi[:, key_tile * VW:(key_tile + 1) * VW]
                    end = g == CH - 1 and j == last
                    pe.matmul(attn_ps[t][:, 0:VW], hi, v, start=(key_tile == 0), stop=False)
                    pe.matmul(attn_ps[t][:, 0:D], hi, v_lo[:, key_tile * VW:key_tile * VW + D], start=False, stop=False)
                    mm = pe.matmul(attn_ps[t][:, 0:VW], lo, v, start=False, stop=end)
                mm.then_inc(values_done, 1)

            def turn_xhat(m, t):
                pe.wait_ge(xhat_ready, m + 1)
                at_least(pe, gates_ready, m)
                for k in range(KC):
                    mm = pe.transpose(rT_ps[:, k], xhat[:, t, k * P:(k + 1) * P], ident[:])
                mm.then_inc(xhat_turned, 1)

            def logits(m):
                pe.wait_ge(router_split, m + 1)
                for k in range(KC):
                    mm = split_product(logits_ps, (rT_hi[:, k], rT_lo[:, k]), (rwT_hi[:, k], rwT_lo[:, k]),
                                       k == 0, k == KC - 1)
                mm.then_inc(logits_ready, 1)

            def ranks(m):
                pe.wait_ge(picks_ready, m + 1)
                pe.matmul(rank_ps, before[:], picked[:], start=True, stop=True)
                pe.matmul(total_ps, ones[:], picked[:], start=True, stop=True).then_inc(ranks_ready, 1)

            def step(n, t, next_block=None, new=True, old=True, post=True):
                m, u = n - 1, 1 - t
                for g in range(CH + 2):
                    if new and g < CH:
                        scores(n, t, g)
                    if next_block is not None and g == 2:
                        queries(next_block)
                    if old and 1 <= g <= CH:
                        turn_probs(m, u, g - 1)
                    if post and g == 3:
                        turn_xhat(n - 2, t)
                    if post and g == 5:
                        logits(n - 2)
                    if old and g >= 2:
                        values(m, u, g - 2)
                    if post and g == CH:
                        ranks(n - 2)

            pe.wait_ge(stage_kept, 2)
            queries(0)
            pe.wait_ge(stage_kept, TILES)
            pe.wait_ge(v_split, TILES)
            pe.wait_ge(v_columns_made, 2)
            step(0, 0, old=False, post=False)
            step(1, 1, next_block=1, post=False)
            step(2, 0)
            with pe.Fori(1, BLOCKS - 1) as b:
                step(2 * b + 1, 1, next_block=b + 1)
                step(2 * b + 2, 0)
            step(TILES - 1, 1)
            step(TILES, 0, new=False)
            step(TILES + 1, 1, new=False, old=False)

            for i in range(2 * FP):
                ps = hidden_ps[i % 4]
                at_least(pe, w_split, i - 3)
                if i == 0:
                    pe.wait_ge(w1_in, 16)
                if i == FP:
                    pe.wait_ge(w2_in, 16)
                for j in range(4):
                    if i < FP:
                        src = w1nat[:, 4 * (i % 2) + j, (i // 2) * P:(i // 2 + 1) * P]
                    else:
                        f = 2 * (i - FP) + j // 2
                        src = w2nat[:, j % 2, f * P:(f + 1) * P]
                    mm = pe.transpose(ps[:, j * P:(j + 1) * P], src, ident[:])
                mm.then_inc(w_turned, 1)

            def turn_fx(b):
                pe.wait_ge(fx_ready, b + 1)
                at_least(pe, fx_split, b)
                for k in range(KC):
                    for t in range(2):
                        mm = pe.transpose(qT_ps[:, k, t * P:(t + 1) * P], xhat[:, t, k * P:(k + 1) * P], ident[:])
                mm.then_inc(fx_turned, 1)

            def hidden(b):
                pe.wait_ge(fx_split, b + 1)
                for p in range(FP):
                    at_least(pe, gelu_done, FP * (b - 1) + p + 1)
                    for i in range(2):
                        f = slice((2 * p + i) * P, (2 * p + i + 1) * P)
                        for k in range(KC):
                            mm = split_product(hidden_ps[p][:, i * B:(i + 1) * B],
                                               (w1T[0][:, k, f], w1T[1][:, k, f]),
                                               (qT_hi[:, k], qT_lo[:, k]), k == 0, k == KC - 1)
                    mm.then_inc(hidden_ready, 1)

            def output(b):
                at_least(pe, y_taken, 2 * b)
                for p in range(FP):
                    pe.wait_ge(hidden_split, FP * b + p + 1)
                    for i in range(2):
                        f = 2 * p + i
                        for t in range(2):
                            cols = slice(t * P, (t + 1) * P)
                            mm = split_product(y_ps[t][:, 0:D], (hT_hi[:, f, cols], hT_lo[:, f, cols]),
                                               (w2T[0][:, f], w2T[1][:, f]), f == 0, f == FT - 1)
                    mm.then_inc(hidden_used, 1)

            turn_fx(0)
            pe.wait_ge(w_split, 2 * FP)
            hidden(0)
            turn_fx(1)
            output(0)
            with pe.Fori(1, BLOCKS - 1) as b:
                hidden(b)
                turn_fx(b + 1)
                output(b)
            hidden(BLOCKS - 1)
            output(BLOCKS - 1)

        @block.scalar
        def _(act):
            a = nc.scalar
            act.dma_start(wnat[:, 0], Wq.rearrange("(k p) d -> p k d", p=P)).then_inc(weights_in, 16)
            act.dma_start(wnat[:, 1], Wk.rearrange("(k p) d -> p k d", p=P)).then_inc(weights_in, 16)
            act.dma_start(wnat[:, 2], Wv.rearrange("(k p) d -> p k d", p=P)).then_inc(weights_in, 16)
            act.dma_start(rwnat, router_w).then_inc(weights_in, 16)
            act.dma_start(b1_sb[:], b1.rearrange("(f p) -> p f", p=P), allow_slow_non_contiguous=True) \
                .then_inc(biases_in, 16)
            act.dma_start(b2_sb[:], b2.rearrange("(o d) -> o d", o=1).broadcast_to([P, D])).then_inc(biases_in, 16)

            def copy(dst, src):
                return a.activation(dst, src, ACT.Copy)

            act.wait_ge(a_ready, 1)
            copy(a_hi[:], qT_ps).then_inc(a_hi_out, 1)
            act.wait_ge(a_ready, 2)
            copy(wvT_hi, attn_ps[0][:].rearrange("p (k d) -> p k d", k=KC)).then_inc(a_hi_out, 1)
            act.wait_ge(a_ready, 3)
            copy(rwT_hi[:], route_ps[:, 0:KC * E].rearrange("p (k e) -> p k e", k=KC)).then_inc(a_hi_out, 1)

            def prep_stage(m, t):
                act.wait_ge(xn_turned, m + 1)
                at_least(act, v_ready, m - 1)
                at_least(act, stage_kept, m - 1)
                copy(qT_hi[:, :, t * P:(t + 1) * P],
                     turn_ps[t][:, 0:KC * P].rearrange("p (k t) -> p k t", k=KC)).then_inc(stage_hi, 1)

            def prep_v(m, t):
                act.wait_ge(v_ready, m + 1)
                copy(v_hi[:, ds(m * VW, D)], score_ps[t][:, 0:D]).then_inc(v_hi_out, 1)

            prep_stage(0, 0)
            prep_stage(1, 1)
            prep_v(0, 0)
            with act.Fori(1, BLOCKS) as b:
                prep_stage(2 * b, 0)
                prep_v(2 * b - 1, 1)
                prep_stage(2 * b + 1, 1)
                prep_v(2 * b, 0)
            prep_v(TILES - 1, 1)

            def queries_hi(n, h, b):
                act.wait_ge(q_ready, b + 1)
                at_least(act, q_split, n)
                at_least(act, scores_ready, CH * (n - 1))
                copy(qT_hi[:, :, h * P:(h + 1) * P], qT_ps[:, :, h * P:(h + 1) * P]).then_inc(q_hi_out, 1)

            def exps(m, t):
                act.wait_ge(minus_max_ready, m + 1)
                for part in (probs[:, t, 0:HEAD], probs[:, t, HEAD:KEYS]):
                    a.activation(part, part, ACT.Exp, bias=minus_max[:, t:t + 1]).then_inc(exp_done, 1)

            def probs_hi(m, t, g):
                act.wait_ge(probs_turned, CH * m + g + 1)
                at_least(act, values_done, CH * m + g - 1)
                s = (CH * t + g) % 2
                copy(probsT_hi[:, s, 0:width(g)], turn_ps[s][:, 0:width(g)]).then_inc(probs_hi_out, 1)

            def router_hi(m):
                act.wait_ge(xhat_turned, m + 1)
                at_least(act, logits_ready, m)
                copy(rT_hi[:], rT_ps).then_inc(router_hi_out, 1)

            def router_exps(m):
                act.wait_ge(best_ready, m + 1)
                at_least(act, gates_ready, m)
                a.activation(router_exp[:], logits_sb[:], ACT.Exp, bias=best[:, 1:2],
                             accum_out=router_sum[:]).then_inc(router_exp_done, 1)

            def step(n, t, next_block=None, old=True, post=True):
                if old:
                    exps(n - 1, 1 - t)
                for g in range(CH):
                    if old:
                        probs_hi(n - 1, 1 - t, g)
                    if g == 2 and post:
                        router_hi(n - 2)
                    if g == 2 and next_block is not None:
                        queries_hi(n + 1, 1 - t, next_block)
                    if g == 5 and post:
                        router_exps(n - 2)

            act.wait_ge(v_ready, TILES)
            act.wait_ge(stage_kept, TILES)
            queries_hi(0, 0, 0)
            queries_hi(1, 1, 0)
            step(1, 1, next_block=1, post=False)
            step(2, 0, next_block=1)
            with act.Fori(1, BLOCKS - 1) as b:
                step(2 * b + 1, 1, next_block=b + 1)
                step(2 * b + 2, 0, next_block=b + 1)
            step(TILES - 1, 1)
            step(TILES, 0)
            step(TILES + 1, 1, old=False)

            for i in range(2 * FP):
                act.wait_ge(w_turned, i + 1)
                copy(w_half(i, 0), hidden_ps[i % 4][:]).then_inc(w_hi_out, 1)

            def fx_hi(b):
                act.wait_ge(fx_turned, b + 1)
                at_least(act, hidden_ready, FP * b)
                copy(qT_hi[:], qT_ps).then_inc(fx_hi_out, 1)

            def gelu(b, p):
                act.wait_ge(hidden_ready, FP * b + p + 1)
                at_least(act, hidden_split, FP * (b - 1) + p + 1)
                for i in range(2):
                    f = 2 * p + i
                    ins = a.activation(hT[:, f], hidden_ps[p][:, i * B:(i + 1) * B], ACT.Gelu, bias=b1_sb[:, f:f + 1])
                ins.then_inc(gelu_done, 1)

            def hidden_hi(b, p):
                act.wait_ge(gelu_done, FP * b + p + 1)
                at_least(act, hidden_used, FP * (b - 1) + p + 1)
                copy(hT_hi[:, 2 * p:2 * p + 2], hT[:, 2 * p:2 * p + 2]).then_inc(hidden_hi_out, 1)

            def ffn(b, more=True):
                for p in range(FP + 1):
                    if p < FP:
                        gelu(b, p)
                    if p > 0:
                        hidden_hi(b, p - 1)
                if more:
                    fx_hi(b + 1)

            fx_hi(0)
            act.wait_ge(biases_in, 16 * 2)
            ffn(0)
            with act.Fori(1, BLOCKS - 1) as b:
                ffn(b)
            ffn(BLOCKS - 1, more=False)

        @block.vector
        def _(dve):
            v = nc.vector

            def lo(dst, src, hi):
                return v.tensor_tensor(dst, src, hi, ALU.subtract)

            ones_col = v_hi[:].rearrange("p (t w) -> p t w", t=TILES)[:, :, D:D + 1]
            zero_col = v_hi[:].rearrange("p (t w) -> p t w", t=TILES)[:, :, D + 1:D + 2]
            v.memset(tokens[96:P, (TILES - 1) * D:], 0.0).then_inc(pads_made, 1)
            v.memset(raw[96:P, TILES - 1], 0).then_inc(pads_made, 1)
            v.memset(ones_col.bitcast(F32), 1.0).then_inc(v_columns_made, 1)
            v.memset(zero_col.bitcast(F32), 0.0).then_inc(v_columns_made, 1)
            v.memset(queue[:], 0.0).then_inc(gate_seq, 1)
            dve.wait_ge(x_in[0], 16)
            with dve.Fori(0, 12) as m:
                v.bn_stats(stats[:, ds(m * 6, 6)], tokens[:, tile_of(m)]).then_inc(stats_made, 1)
            dve.wait_ge(x_in[1], 32)
            with dve.Fori(12, TILES) as m:
                v.bn_stats(stats[:, ds(m * 6, 6)], tokens[:, tile_of(m)]).then_inc(stats_made, 1)
            dve.wait_ge(stats_made, TILES)
            st = stats[:].rearrange("p (t s) -> p t s", t=TILES)
            even_mean, even_var, odd_mean, odd_var = st[:, :, 1], st[:, :, 2], st[:, :, 4], st[:, :, 5]
            v.tensor_tensor(mean1[:], even_mean, odd_mean, ALU.add).then_inc(ln_seq, 1)
            v.tensor_tensor(tmp1[:], even_mean, odd_mean, ALU.subtract).then_inc(ln_seq, 1)
            v.tensor_tensor(tmp2[:], even_var, odd_var, ALU.add).then_inc(ln_seq, 1)
            dve.wait_ge(ln_seq, 3)
            v.tensor_scalar(mean1[:], mean1[:], 0.5, None, ALU.mult).then_inc(ln_seq, 1)
            v.scalar_tensor_tensor(out=tmp1[:], in0=tmp1[:], scalar=0.25, in1=tmp1[:], op0=ALU.mult,
                                   op1=ALU.mult).then_inc(ln_seq, 1)
            v.tensor_scalar(tmp2[:], tmp2[:], 1.0 / D, EPS, ALU.mult, ALU.add).then_inc(ln_seq, 1)
            dve.wait_ge(ln_seq, 6)
            v.tensor_tensor(rstd1[:], tmp1[:], tmp2[:], ALU.add).then_inc(var1_ready, 1)

            def normalise(dst, m, mean, rstd):
                return v.tensor_scalar(dst, tokens[:, tile_of(m)], mean[:, ds(m, 1)], rstd[:, ds(m, 1)],
                                       ALU.subtract, ALU.mult)

            def prep_xn(m, t):
                at_least(dve, xn_turned, m - 1)
                normalise(xhat[:, t], m, mean1, rstd1).then_inc(xn_ready, 1)

            def prep_stage(m, t):
                dve.wait_ge(stage_hi, m + 1)
                cols = slice(t * P, (t + 1) * P)
                lo(qT_lo[:, :, cols], turn_ps[t][:, 0:KC * P].rearrange("p (k t) -> p k t", k=KC),
                   qT_hi[:, :, cols]).then_inc(stage_split, 1)

            def prep_v(m, t):
                dve.wait_ge(v_hi_out, m + 1)
                lo(v_lo[:, ds(m * VW, D)], score_ps[t][:, 0:D], v_hi[:, ds(m * VW, D)]).then_inc(v_split, 1)

            dve.wait_ge(rstd1_ready, 1)
            prep_xn(0, 0)
            dve.wait_ge(a_hi_out, 1)
            lo(a_lo[:], qT_ps, a_hi[:]).then_inc(a_split, 1)
            dve.wait_ge(a_hi_out, 2)
            lo(wvT_lo, attn_ps[0][:].rearrange("p (k d) -> p k d", k=KC), wvT_hi).then_inc(a_split, 1)
            dve.wait_ge(a_hi_out, 3)
            lo(rwT_lo[:], route_ps[:, 0:KC * E].rearrange("p (k e) -> p k e", k=KC), rwT_hi[:]).then_inc(a_split, 1)
            prep_xn(1, 1)
            prep_stage(0, 0)
            prep_xn(2, 0)
            prep_stage(1, 1)
            prep_v(0, 0)
            with dve.Fori(1, BLOCKS - 1) as b:
                for t in range(2):
                    m = 2 * b + t
                    prep_xn(m + 1, 1 - t)
                    prep_stage(m, t)
                    prep_v(m - 1, 1 - t)
            prep_xn(TILES - 1, 1)
            prep_stage(TILES - 2, 0)
            prep_v(TILES - 3, 1)
            prep_stage(TILES - 1, 1)
            prep_v(TILES - 2, 0)
            prep_v(TILES - 1, 1)

            def queries_lo(n, h):
                dve.wait_ge(q_hi_out, n + 1)
                cols = slice(h * P, (h + 1) * P)
                lo(qT_lo[:, :, cols], qT_ps[:, :, cols], qT_hi[:, :, cols]).then_inc(q_split, 1)

            def mask(n, h, b):
                dve.wait_ge(adj_in, 32 * b + 32)
                at_least(dve, scores_ready, CH * (n - 1))
                cols = slice(h * P // 4, (h + 1) * P // 4)
                words = [s.bitcast(U32)[:, :, cols] for s in (missing, raw)]
                v.tensor_scalar(words[0], words[1], 0x01010101, NO_EDGE_BYTE_SHIFT, ALU.bitwise_xor,
                                ALU.logical_shift_left).then_inc(mask_ready, 1)

            def take_scores(n, t, g):
                dve.wait_ge(scores_ready, CH * n + g + 1)
                if g == 0:
                    at_least(dve, probs_turned, CH * (n - 1))
                w = width(g)
                v.tensor_scalar(probs[:, t, g * CHUNK:g * CHUNK + w], score_ps[(CH * t + g) % 2][:, 0:w],
                                0.0, None, ALU.add, ALU.max, accum_out=chunk_max[:, t, g:g + 1]) \
                    .then_inc(scores_taken, 1)

            def maximum(n, t):
                dve.wait_ge(scores_taken, CH * (n + 1))
                v.tensor_reduce(row_max[:, t:t + 1], chunk_max[:, t], AX.X, ALU.max).then_inc(max_seq, 1)
                dve.wait_ge(max_seq, n + 1)
                v.tensor_scalar(minus_max[:, t:t + 1], row_max[:, t:t + 1], -1.0, None, ALU.mult) \
                    .then_inc(minus_max_ready, 1)
                v.tensor_scalar(has_edge[:, t:t + 1], row_max[:, t:t + 1], NO_EDGE / 2, None, ALU.is_gt)

            def probs_lo(m, t, g):
                dve.wait_ge(probs_hi_out, CH * m + g + 1)
                s = (CH * t + g) % 2
                w = width(g)
                lo(probsT_lo[:, s, 0:w], turn_ps[s][:, 0:w], probsT_hi[:, s, 0:w]).then_inc(probs_split, 1)

            def finish(m, t):
                seq = FINISH_STEPS * m

                def link(ins, k):
                    ins.then_inc(finish_seq, 1)
                    dve.wait_ge(finish_seq, seq + k)

                dve.wait_ge(values_done, CH * (m + 1))
                link(v.reciprocal(inv_sum[:, t:t + 1], attn_ps[t][:, D:D + 1]), 1)
                link(v.tensor_tensor(row_scale[:, t:t + 1], inv_sum[:, t:t + 1], has_edge[:, t:t + 1], ALU.mult), 2)
                v.scalar_tensor_tensor(out=tokens[:, tile_of(m)], in0=attn_ps[t][:, 0:D], scalar=row_scale[:, t:t + 1],
                                       in1=tokens[:, tile_of(m)], op0=ALU.mult, op1=ALU.add).then_inc(attn_taken, 1)
                wait_apart(dve, attn_taken, m + 1)
                link(v.bn_stats(stats2[:], tokens[:, tile_of(m)]), 3)
                dve.sem_inc(waited_apart, 1)
                link(v.bn_aggr(meanvar2[:], stats2[:]), 4)
                at_least(dve, rstd2_ready, m)
                v.tensor_scalar(var_eps[:], meanvar2[:, 1:2], EPS, None, ALU.add).then_inc(var2_ready, 1)
                link(v.tensor_copy(mean2[:, ds(m, 1)], meanvar2[:, 0:1]), 5)

            def second_norm(m, t):
                dve.wait_ge(rstd2_ready, m + 1)
                dve.wait_ge(finish_seq, FINISH_STEPS * (m + 1))
                at_least(dve, xhat_turned, m - 1)
                normalise(xhat[:, t], m, mean2, rstd2).then_inc(xhat_ready, 1)

            def router_lo(m):
                dve.wait_ge(router_hi_out, m + 1)
                lo(rT_lo[:], rT_ps, rT_hi[:]).then_inc(router_split, 1)

            def pick(m):
                seq = ROUTE_STEPS * m

                def link(ins, k):
                    ins.then_inc(route_seq, 1)
                    dve.wait_ge(route_seq, seq + k)

                dve.wait_ge(logits_ready, m + 1)
                at_least(dve, router_exp_done, m)
                link(v.tensor_copy(logits_sb[:], logits_ps), 1)
                link(v.tensor_reduce(best[:, 0:1], logits_sb[:], AX.X, ALU.max), 2)
                v.tensor_scalar(best[:, 1:2], best[:, 0:1], -1.0, None, ALU.mult).then_inc(best_ready, 1)
                link(v.scalar_tensor_tensor(out=cand[:], in0=logits_sb[:], scalar=best[:, 0:1], in1=rev[:],
                                            op0=ALU.is_equal, op1=ALU.mult), 3)
                link(v.tensor_reduce(best[:, 2:3], cand[:], AX.X, ALU.max), 4)
                link(v.tensor_scalar(first[:], rev[:], best[:, 2:3], None, ALU.is_equal), 5)
                link(v.scalar_tensor_tensor(out=rest[:], in0=first[:], scalar=-BIG, in1=logits_sb[:],
                                            op0=ALU.mult, op1=ALU.add), 6)
                link(v.tensor_reduce(best[:, 3:4], rest[:], AX.X, ALU.max), 7)
                v.scalar_tensor_tensor(out=cand[:], in0=rest[:], scalar=best[:, 3:4], in1=rev[:],
                                       op0=ALU.is_equal, op1=ALU.mult).then_inc(route_seq, 1)
                dve.wait_ge(route_seq, seq + ROUTE_STEPS)
                v.tensor_reduce(best[:, 4:5], cand[:], AX.X, ALU.max).then_inc(gate_seq, 1)
                dve.wait_ge(gate_seq, 1 + GATE_STEPS * m + 1)
                at_least(dve, ranks_ready, m)
                v.scalar_tensor_tensor(out=picked[:], in0=rev[:], scalar=best[:, 4:5], in1=first[:],
                                       op0=ALU.is_equal, op1=ALU.add).then_inc(picks_ready, 1)

            def gate(m):
                seq = 1 + GATE_STEPS * m + 1
                dve.wait_ge(ranks_ready, m + 1)
                dve.wait_ge(router_exp_done, m + 1)
                v.tensor_tensor(rank[:], rank_ps, queue[:], ALU.add).then_inc(gate_seq, 1)
                v.reciprocal(best[:, 5:6], router_sum[:])
                dve.wait_ge(gate_seq, seq + 1)
                v.tensor_tensor(queue[:], total_ps, queue[:], ALU.add)
                v.scalar_tensor_tensor(out=kept[:], in0=rank[:], scalar=float(CAPACITY), in1=picked[:],
                                       op0=ALU.is_lt, op1=ALU.mult).then_inc(gate_seq, 1)
                dve.wait_ge(gate_seq, seq + 2)
                v.tensor_tensor_reduce(cand[:], kept[:], router_exp[:], 1.0, 0.0, ALU.mult, ALU.add,
                                       best[:, 6:7]).then_inc(gate_seq, 1)
                dve.wait_ge(gate_seq, seq + 3)
                v.tensor_tensor(gates[:, ds(m, 1)], best[:, 6:7], best[:, 5:6], ALU.mult).then_inc(gates_ready, 1)

            def step(n, t, next_block=None, mask_block=None, new=True, old=True, post=True):
                m, u = n - 1, 1 - t
                for g in range(CH + 1):
                    if new and g < CH:
                        take_scores(n, t, g)
                    if new and g == CH - 1:
                        maximum(n, t)
                        if mask_block is not None:
                            mask(n + 2, t, mask_block)
                    if post and g == 1:
                        second_norm(n - 2, t)
                    if old and 1 <= g:
                        probs_lo(m, u, g - 1)
                    if g == 3 and post:
                        router_lo(n - 2)
                    if g == 3 and next_block is not None:
                        queries_lo(n + 1, u)
                    if post and g == CH - 1:
                        pick(n - 2)
                if post:
                    gate(n - 2)
                if old:
                    finish(m, u)

            mask(0, 0, 0)
            mask(1, 1, 0)
            queries_lo(0, 0)
            queries_lo(1, 1)
            step(0, 0, mask_block=1, old=False, post=False)
            step(1, 1, next_block=1, mask_block=1, post=False)
            step(2, 0, next_block=1, mask_block=2)
            with dve.Fori(1, BLOCKS - 2) as b:
                step(2 * b + 1, 1, next_block=b + 1, mask_block=b + 1)
                step(2 * b + 2, 0, next_block=b + 1, mask_block=b + 2)
            step(TILES - 3, 1, next_block=BLOCKS - 1, mask_block=BLOCKS - 1)
            step(TILES - 2, 0, next_block=BLOCKS - 1)
            step(TILES - 1, 1)
            step(TILES, 0, new=False)
            step(TILES + 1, 1, new=False, old=False)

            for i in range(2 * FP):
                dve.wait_ge(w_hi_out, i + 1)
                lo(w_half(i, 1), hidden_ps[i % 4][:], w_half(i, 0)).then_inc(w_split, 1)

            def fx_norm(b):
                at_least(dve, fx_turned, b)
                normalise(xhat[:, 0], 2 * b, mean2, rstd2)
                normalise(xhat[:, 1], 2 * b + 1, mean2, rstd2).then_inc(fx_ready, 1)

            def fx_lo(b):
                dve.wait_ge(fx_hi_out, b + 1)
                lo(qT_lo[:], qT_ps, qT_hi[:]).then_inc(fx_split, 1)

            def ffn(b, more=True):
                if more:
                    fx_norm(b + 1)
                for p in range(FP):
                    dve.wait_ge(hidden_hi_out, FP * b + p + 1)
                    pair = slice(2 * p, 2 * p + 2)
                    lo(hT_lo[:, pair], hT[:, pair], hT_hi[:, pair]).then_inc(hidden_split, 1)
                if more:
                    fx_lo(b + 1)
                dve.wait_ge(hidden_used, FP * (b + 1))
                for t in range(2):
                    v.tensor_tensor(y_sb[:, t], y_ps[t][:, 0:D], b2_sb[:], ALU.add).then_inc(y_taken, 1)
                for t in range(2):
                    m = 2 * b + t
                    dve.wait_ge(y_taken, m + 1)
                    v.scalar_tensor_tensor(out=tokens[:, tile_of(m)], in0=y_sb[:, t], scalar=gates[:, ds(m, 1)],
                                           in1=tokens[:, tile_of(m)], op0=ALU.mult, op1=ALU.add) \
                        .then_inc(out_ready, 1)

            dve.wait_ge(xhat_turned, TILES)
            dve.wait_ge(gates_ready, TILES)
            fx_norm(0)
            fx_lo(0)
            dve.wait_ge(biases_in, 16 * 2)
            ffn(0)
            with dve.Fori(1, BLOCKS - 1) as b:
                ffn(b)
            ffn(BLOCKS - 1, more=False)


_INS = ["x", "adj", "L0_gnn_Wq", "L0_gnn_Wk", "L0_gnn_Wv", "L0_ffn_router_w", "L0_ffn_w1", "L0_ffn_b1",
        "L0_ffn_w2", "L0_ffn_b2"]


def kernel(**inputs):
    import numpy as _np
    import concourse.bacc as _bacc
    from concourse import mybir as _mybir
    from concourse.bass_utils import run_bass_kernel_spmd as _run

    nc = _bacc.Bacc("TRN2", target_bir_lowering=False, num_devices=1)
    arrays, args = {}, []
    for name in _INS:
        a = _np.ascontiguousarray(inputs[name])
        arrays[f"in_{name}_dram"] = a
        args.append(nc.dram_tensor(f"in_{name}_dram", a.shape, _mybir.dt.from_np(a.dtype), kind="ExternalInput").ap())
    shape = inputs["x"].shape
    args.append(nc.dram_tensor("out_dram", shape, _mybir.dt.float32, kind="ExternalOutput").ap())
    build(nc, *args)
    r = _run(nc, [arrays], core_ids=[0])
    return r.results[0]["out_dram"]
```

```python
from contextlib import ExitStack

import concourse.bass as bass
from concourse import mybir

ACT = mybir.ActivationFunctionType
ALU = mybir.AluOpType
AX = mybir.AxisListType
F32 = mybir.dt.float32
F32R = mybir.dt.float32r
BF16 = mybir.dt.bfloat16
U8 = mybir.dt.uint8

P = 128
EPS = 1e-5
CAPACITY = 256
NO_EDGE = -1e30
BIG = 3e38


def ds(start, size):
    return bass.ds(start, size)


def at_least(engine, semaphore, value):
    if not isinstance(value, int) or value > 0:
        engine.wait_ge(semaphore, value)


def build(nc, x, edges, Wq, Wk, WvT, router_wT, w1T_in, b1, w2T_in, b2, out):
    N, D = x.shape
    E = router_wT.shape[1]
    F = w1T_in.shape[1]
    TILES = N // P
    BLOCKS = TILES // 2
    KEYS = TILES * P
    KC = D // P
    B = 2 * P
    CHUNK = 512
    CH = (KEYS + CHUNK - 1) // CHUNK
    FT = F // P
    FP = FT // 2
    VW = D + 2
    HEAD = 2 * CHUNK
    assert TILES == 2 * BLOCKS and BLOCKS > 3 and D == 256 and F % B == 0

    def width(g):
        return min(CHUNK, KEYS - g * CHUNK)

    with ExitStack() as ctx:
        def sb(name, shape, dt):
            return ctx.enter_context(nc.sbuf_tensor(name, shape, dt))

        def sem(name):
            return ctx.enter_context(nc.semaphore(name))

        GROUPS = [(0, 2)] + [(m, m + 4) for m in range(2, TILES, 4)]

        tokens = sb("tokens", [P, TILES * D], F32)
        xnT_hi = sb("xnT_hi", [P, KC, KEYS], F32R)
        xnT_lo = sb("xnT_lo", [P, KC, KEYS], F32R)
        v_hi = sb("v_hi", [P, TILES * VW], F32R)
        v_lo = sb("v_lo", [P, TILES * VW], F32R)
        probs = sb("probs", [P, 2, KEYS], F32)
        probsT_hi = sb("probsT_hi", [P, 2, CHUNK], F32R)
        probsT_lo = sb("probsT_lo", [P, 2, CHUNK], F32R)
        edges_sb = sb("edges_sb", [P, KEYS], U8)
        no_edge = sb("no_edge", [P, 2, KEYS], BF16)
        qT_hi = sb("qT_hi", [P, KC, B], F32R)
        qT_lo = sb("qT_lo", [P, KC, B], F32R)
        a_hi = sb("a_hi", [P, KC, D], F32R)
        a_lo = sb("a_lo", [P, KC, D], F32R)
        xhat = sb("xhat", [P, 2, D], F32)
        rT_hi = sb("rT_hi", [P, KC, P], F32R)
        rT_lo = sb("rT_lo", [P, KC, P], F32R)
        rwT_hi = sb("rwT_hi", [P, KC, E], F32R)
        rwT_lo = sb("rwT_lo", [P, KC, E], F32R)
        ident = sb("ident", [P, P], F32)
        before = sb("before", [P, P], BF16)
        ones = sb("ones", [P, P], BF16)
        rev = sb("rev", [P, E], F32)
        minus_half = sb("minus_half", [P, TILES], F32)
        stats = sb("stats", [P, TILES * 6], F32)
        mean1 = sb("mean1", [P, TILES], F32)
        rstd1 = sb("rstd1", [P, TILES], F32)
        mean2 = sb("mean2", [P, TILES], F32)
        rstd2 = sb("rstd2", [P, TILES], F32)
        gates = sb("gates", [P, TILES], F32)
        tmp1 = sb("tmp1", [P, TILES], F32)
        tmp2 = sb("tmp2", [P, TILES], F32)
        shift1 = sb("shift1", [P, TILES], F32)
        chunk_max = sb("chunk_max", [P, 2, CH], F32)
        row_max = sb("row_max", [P, 2], F32)
        minus_max = sb("minus_max", [P, 2], F32)
        has_edge = sb("has_edge", [P, 2], F32)
        inv_sum = sb("inv_sum", [P, 2], F32)
        row_scale = sb("row_scale", [P, 2], F32)
        stats2 = sb("stats2", [P, 6], F32)
        meanvar2 = sb("meanvar2", [P, 2], F32)
        var_eps = sb("var_eps", [P, 1], F32)
        best = sb("best", [P, 8], F32)
        cand = sb("cand", [P, E], F32)
        first = sb("first", [P, E], F32)
        rest = sb("rest", [P, E], F32)
        picked = sb("picked", [P, E], BF16)
        logits_sb = sb("logits_sb", [P, E], F32)
        router_exp = sb("router_exp", [P, E], F32)
        router_sum = sb("router_sum", [P, 1], F32)
        rank = sb("rank", [P, E], F32)
        kept = sb("kept", [P, E], F32)
        queue = sb("queue", [P, E], F32)
        b1_sb = sb("b1_sb", [P, FT], F32)
        b2_sb = sb("b2_sb", [P, D], F32)

        wnat = probs[:, 0, 0:3 * KC * D].rearrange("p (w k d) -> p w k d", w=3, k=KC)
        rwnat = probs[:, 1, 0:KC * E].rearrange("p (k e) -> p k e", k=KC)
        wvT_hi = probsT_hi[:, 0, :].rearrange("p (k d) -> p k d", k=KC)
        wvT_lo = probsT_lo[:, 0, :].rearrange("p (k d) -> p k d", k=KC)
        w1nat = probs[:, 0, 0:KC * F].rearrange("p (k f) -> p k f", k=KC)
        w2nat = no_edge[:].rearrange("p a k -> p (a k)")[:, 0:2 * FT * D].bitcast(F32) \
            .rearrange("p (f d) -> p f d", f=FT)
        w1T = [s[:, 0, 0:KC * F].rearrange("p (k f) -> p k f", k=KC) for s in (xnT_hi, xnT_lo)]
        w2T = [s[:, 1, 0:FT * D].rearrange("p (f d) -> p f d", f=FT) for s in (xnT_hi, xnT_lo)]
        hT = probs[:, 1, 0:FT * B].rearrange("p (f b) -> p f b", f=FT)
        hT_hi = v_hi[:, 0:FT * B].rearrange("p (f b) -> p f b", f=FT)
        hT_lo = v_lo[:, 0:FT * B].rearrange("p (f b) -> p f b", f=FT)
        fx = probs[:, 1, FT * B:FT * B + 2 * D].rearrange("p (t d) -> p t d", t=2)
        y_sb = probs[:, 1, FT * B + 2 * D:FT * B + 4 * D].rearrange("p (t d) -> p t d", t=2)

        def bank(name):
            return ctx.enter_context(nc.psum_tensor(name, [P, CHUNK], F32))

        score_ps = [bank(f"score_ps{i}") for i in range(2)]
        turn_ps = [bank(f"turn_ps{i}") for i in range(2)]
        attn_ps = [bank(f"attn_ps{i}") for i in range(2)]
        q_ps = bank("q_ps")
        route_ps = bank("route_ps")
        qT_ps = q_ps[:].rearrange("p (k b) -> p k b", k=KC)
        rT_ps = route_ps[:, 0:KC * P].rearrange("p (k t) -> p k t", k=KC)
        logits_ps = route_ps[:, 256:256 + E]
        rank_ps = route_ps[:, 320:320 + E]
        total_ps = route_ps[:, 384:384 + E]
        hidden_ps = [*score_ps, *turn_ps]
        y_ps = attn_ps

        weights_in = sem("weights_in")
        biases_in = sem("biases_in")
        x_in = [sem(f"x_in{i}") for i in range(len(GROUPS))]
        edges_in = sem("edges_in")
        consts_made = sem("consts_made")
        zeroed = sem("zeroed")
        v_columns_made = sem("v_columns_made")
        a_ready = sem("a_ready")
        a_hi_out = sem("a_hi_out")
        a_split = sem("a_split")
        stats_made = sem("stats_made")
        ln_seq = sem("ln_seq")
        var1_ready = sem("var1_ready")
        rstd1_ready = sem("rstd1_ready")
        xn_ready = sem("xn_ready")
        xn_turned = sem("xn_turned")
        xn_hi_out = sem("xn_hi_out")
        xn_split = sem("xn_split")
        shift1_ready = sem("shift1_ready")
        v_ready = sem("v_ready")
        v_hi_out = sem("v_hi_out")
        v_split = sem("v_split")
        q_ready = sem("q_ready")
        q_hi_out = sem("q_hi_out")
        q_split = sem("q_split")
        mask_ready = sem("mask_ready")
        scores_ready = sem("scores_ready")
        scores_taken = sem("scores_taken")
        max_seq = sem("max_seq")
        minus_max_ready = sem("minus_max_ready")
        exp_done = sem("exp_done")
        probs_turned = sem("probs_turned")
        probs_hi_out = sem("probs_hi_out")
        probs_split = sem("probs_split")
        values_done = sem("values_done")
        attn_taken = sem("attn_taken")
        finish_seq = sem("finish_seq")
        var2_ready = sem("var2_ready")
        rstd2_ready = sem("rstd2_ready")
        xhat_ready = sem("xhat_ready")
        xhat_turned = sem("xhat_turned")
        router_hi_out = sem("router_hi_out")
        router_split = sem("router_split")
        logits_ready = sem("logits_ready")
        route_seq = sem("route_seq")
        best_ready = sem("best_ready")
        router_exp_done = sem("router_exp_done")
        picks_ready = sem("picks_ready")
        ranks_ready = sem("ranks_ready")
        gate_seq = sem("gate_seq")
        gates_ready = sem("gates_ready")
        w1_in = sem("w1_in")
        w2_in = sem("w2_in")
        w_hi_out = sem("w_hi_out")
        w_split = sem("w_split")
        fx_ready = sem("fx_ready")
        fx_turned = sem("fx_turned")
        fx_hi_out = sem("fx_hi_out")
        fx_split = sem("fx_split")
        hidden_ready = sem("hidden_ready")
        gelu_done = sem("gelu_done")
        hidden_hi_out = sem("hidden_hi_out")
        hidden_split = sem("hidden_split")
        hidden_used = sem("hidden_used")
        y_taken = sem("y_taken")
        out_ready = sem("out_ready")
        stored = sem("stored")
        waited_apart = sem("waited_apart")

        FINISH_STEPS, ROUTE_STEPS, GATE_STEPS = 5, 9, 3
        block = ctx.enter_context(nc.Block())

        def group_of(m):
            return next(i for i, (first_tile, end) in enumerate(GROUPS) if m < end)

        def wait_apart(engine, semaphore, value):
            at_least(engine, semaphore, value)
            engine.sem_inc(waited_apart, 1)

        def tile_of(m):
            return ds(m * D, D)

        @block.sync
        def _(sp):
            for (first_tile, end), landed in zip(GROUPS, x_in):
                sp.dma_start(tokens[:, first_tile * D:end * D].rearrange("p (t d) -> p t d", d=D),
                             x[first_tile * P:end * P].rearrange("(t p) d -> p t d", p=P)).then_inc(landed, 16)

            def load_edges(n):
                wait_apart(sp, mask_ready, n)
                sp.dma_start(edges_sb[:], edges[ds(n * P, P)]).then_inc(edges_in, 16)

            load_edges(0)
            with sp.Fori(1, TILES) as n:
                load_edges(n)

            sp.wait_ge(probs_turned, CH * (TILES - 1))
            sp.dma_start(w1nat, w1T_in.rearrange("(k p) f -> p k f", p=P)).then_inc(w1_in, 16)
            sp.wait_ge(scores_taken, CH * TILES)
            sp.dma_start(w2nat, w2T_in.rearrange("(f p) d -> p f d", p=P)).then_inc(w2_in, 16)

            with sp.Fori(0, BLOCKS) as b:
                wait_apart(sp, out_ready, 2 * b + 2)
                sp.dma_start(out[ds(b * B, B)].rearrange("(t p) d -> p t d", p=P),
                             tokens[:, ds(b * 2 * D, 2 * D)].rearrange("p (t d) -> p t d", t=2)) \
                    .then_inc(stored, 16)
            sp.wait_ge(stored, 16 * BLOCKS)

        @block.gpsimd
        def _(pool):
            g = nc.gpsimd
            g.memset(ident[:], 0.0).then_inc(zeroed, 1)
            g.memset(before[:], 0.0).then_inc(zeroed, 1)
            g.memset(ones[:], 1.0).then_inc(consts_made, 1)
            g.memset(minus_half[:], -0.5).then_inc(consts_made, 1)
            pool.wait_ge(zeroed, 2)
            g.affine_select(out=ident[:], in_=ident[:], compare_op=ALU.not_equal, fill=1.0, base=0,
                            pattern=[[-1, P]], channel_multiplier=1).then_inc(consts_made, 1)
            g.affine_select(out=before[:], in_=before[:], compare_op=ALU.is_ge, fill=1.0, base=0,
                            pattern=[[-1, P]], channel_multiplier=1).then_inc(consts_made, 1)
            g.iota(rev[:], pattern=[[-1, E]], base=E, channel_multiplier=0,
                   allow_small_or_imprecise_dtypes=True).then_inc(consts_made, 1)

            pool.wait_ge(consts_made, 5)
            def power(i):
                cols = slice(*GROUPS[i])
                pool.wait_ge(var1_ready, i + 1)
                g.tensor_tensor(rstd1[:, cols], rstd1[:, cols], minus_half[:, cols], ALU.pow) \
                    .then_inc(rstd1_ready, 1)

            for i in range(len(GROUPS)):
                power(i)

            with pool.Fori(0, TILES) as m:
                pool.wait_ge(var2_ready, m + 1)
                g.tensor_tensor(rstd2[:, ds(m, 1)], var_eps[:], minus_half[:, 0:1], ALU.pow) \
                    .then_inc(rstd2_ready, 1)

        @block.tensor
        def _(pe):
            def split_product(out_ps, lhs, rhs, start, stop):
                pe.matmul(out_ps, lhs[0], rhs[0], start=start, stop=False)
                pe.matmul(out_ps, lhs[0], rhs[1], start=False, stop=False)
                return pe.matmul(out_ps, lhs[1], rhs[0], start=False, stop=stop)

            pe.wait_ge(consts_made, 5)
            def prep_turn(m):
                pe.wait_ge(xn_ready, m + 1)
                at_least(pe, xn_split, m - 1)
                for k in range(KC):
                    mm = pe.transpose(turn_ps[m % 2][:, k * P:(k + 1) * P], xhat[:, m % 2, k * P:(k + 1) * P], ident[:])
                mm.then_inc(xn_turned, 1)

            def prep_v(m):
                pe.wait_ge(xn_split, m + 1)
                at_least(pe, v_split, m - 1)
                for k in range(KC):
                    tile = slice(m * P, (m + 1) * P)
                    mm = split_product(score_ps[m % 2][:, 0:D], (xnT_hi[:, k, tile], xnT_lo[:, k, tile]),
                                       (wvT_hi[:, k], wvT_lo[:, k]), k == 0, k == KC - 1)
                mm.then_inc(v_ready, 1)

            prep_turn(0)
            pe.wait_ge(weights_in, 16 * 4)
            for m in range(KC):
                for k in range(KC):
                    mm = pe.matmul(qT_ps[:, m], wnat[:, 0, k, m * P:(m + 1) * P], wnat[:, 1, k],
                                   start=(k == 0), stop=(k == KC - 1))
            mm.then_inc(a_ready, 1)
            pe.wait_ge(a_split, 2)
            for m in range(1, TILES):
                prep_turn(m)
                prep_v(m - 1)
            prep_v(TILES - 1)

            def queries(b):
                at_least(pe, q_split, 2 * b)
                for m in range(KC):
                    for k in range(KC):
                        cols = ds(b * B, B)
                        mm = split_product(qT_ps[:, m], (a_hi[:, k, m * P:(m + 1) * P], a_lo[:, k, m * P:(m + 1) * P]),
                                           (xnT_hi[:, k, cols], xnT_lo[:, k, cols]), k == 0, k == KC - 1)
                mm.then_inc(q_ready, 1)

            def scores(n, t, g):
                if g == 0:
                    pe.wait_ge(q_split, n + 1)
                at_least(pe, scores_taken, CH * n + g - 1)
                ps = score_ps[(CH * t + g) % 2]
                w = width(g)
                for k in range(KC):
                    q = (qT_hi[:, k, t * P:(t + 1) * P], qT_lo[:, k, t * P:(t + 1) * P])
                    keys = slice(g * CHUNK, g * CHUNK + w)
                    mm = split_product(ps[:, 0:w], q, (xnT_hi[:, k, keys], xnT_lo[:, k, keys]), k == 0, k == KC - 1)
                mm.then_inc(scores_ready, 1)

            def turn_probs(m, t, g):
                if g in (0, HEAD // CHUNK):
                    pe.wait_ge(exp_done, 2 * m + 1 + (g > 0))
                at_least(pe, probs_split, CH * m + g - 1)
                ps = turn_ps[(CH * t + g) % 2]
                for j in range(width(g) // P):
                    at = g * CHUNK + j * P
                    mm = pe.transpose(ps[:, j * P:(j + 1) * P], probs[:, t, at:at + P], ident[:])
                mm.then_inc(probs_turned, 1)

            def values(m, t, g):
                pe.wait_ge(probs_split, CH * m + g + 1)
                if g == 0:
                    at_least(pe, attn_taken, m - 1)
                s = (CH * t + g) % 2
                last = width(g) // P - 1
                for j in range(last + 1):
                    key_tile = g * (CHUNK // P) + j
                    hi, lo = probsT_hi[:, s, j * P:(j + 1) * P], probsT_lo[:, s, j * P:(j + 1) * P]
                    v = v_hi[:, key_tile * VW:(key_tile + 1) * VW]
                    end = g == CH - 1 and j == last
                    pe.matmul(attn_ps[t][:, 0:VW], hi, v, start=(key_tile == 0), stop=False)
                    pe.matmul(attn_ps[t][:, 0:D], hi, v_lo[:, key_tile * VW:key_tile * VW + D], start=False, stop=False)
                    mm = pe.matmul(attn_ps[t][:, 0:VW], lo, v, start=False, stop=end)
                mm.then_inc(values_done, 1)

            def turn_xhat(m, t):
                pe.wait_ge(xhat_ready, m + 1)
                at_least(pe, gates_ready, m)
                for k in range(KC):
                    mm = pe.transpose(rT_ps[:, k], xhat[:, t, k * P:(k + 1) * P], ident[:])
                mm.then_inc(xhat_turned, 1)

            def logits(m):
                pe.wait_ge(router_split, m + 1)
                for k in range(KC):
                    mm = split_product(logits_ps, (rT_hi[:, k], rT_lo[:, k]), (rwT_hi[:, k], rwT_lo[:, k]),
                                       k == 0, k == KC - 1)
                mm.then_inc(logits_ready, 1)

            def ranks(m):
                pe.wait_ge(picks_ready, m + 1)
                pe.matmul(rank_ps, before[:], picked[:], start=True, stop=True)
                pe.matmul(total_ps, ones[:], picked[:], start=True, stop=True).then_inc(ranks_ready, 1)

            def step(n, t, next_block=None, new=True, old=True, post=True, late=True):
                m, u = n - 1, 1 - t
                for g in range(CH + 2):
                    if new and g < CH:
                        scores(n, t, g)
                    if next_block is not None and g == 2:
                        queries(next_block)
                    if old and 1 <= g <= CH:
                        turn_probs(m, u, g - 1)
                    if late and g == 1:
                        ranks(n - 3)
                    if post and g == 4:
                        turn_xhat(n - 2, t)
                    if post and g == 6:
                        logits(n - 2)
                    if old and g >= 2:
                        values(m, u, g - 2)

            pe.wait_ge(a_split, 3)
            queries(0)
            pe.wait_ge(v_split, TILES)
            pe.wait_ge(v_columns_made, 2)
            step(0, 0, old=False, post=False, late=False)
            step(1, 1, next_block=1, post=False, late=False)
            step(2, 0, late=False)
            with pe.Fori(1, BLOCKS - 1) as b:
                step(2 * b + 1, 1, next_block=b + 1)
                step(2 * b + 2, 0)
            step(TILES - 1, 1)
            step(TILES, 0, new=False)

            def turn_fx(b):
                pe.wait_ge(fx_ready, b + 1)
                at_least(pe, fx_split, b)
                for k in range(KC):
                    for t in range(2):
                        mm = pe.transpose(qT_ps[:, k, t * P:(t + 1) * P], fx[:, t, k * P:(k + 1) * P], ident[:])
                mm.then_inc(fx_turned, 1)

            def hidden(b):
                pe.wait_ge(fx_split, b + 1)
                for p in range(FP):
                    at_least(pe, gelu_done, FP * (b - 1) + p + 1)
                    for i in range(2):
                        f = slice((2 * p + i) * P, (2 * p + i + 1) * P)
                        for k in range(KC):
                            mm = split_product(hidden_ps[p][:, i * B:(i + 1) * B],
                                               (w1T[0][:, k, f], w1T[1][:, k, f]),
                                               (qT_hi[:, k], qT_lo[:, k]), k == 0, k == KC - 1)
                    mm.then_inc(hidden_ready, 1)

            def output(b):
                at_least(pe, y_taken, 2 * b)
                for p in range(FP):
                    pe.wait_ge(hidden_split, FP * b + p + 1)
                    for i in range(2):
                        f = 2 * p + i
                        for t in range(2):
                            cols = slice(t * P, (t + 1) * P)
                            mm = split_product(y_ps[t][:, 0:D], (hT_hi[:, f, cols], hT_lo[:, f, cols]),
                                               (w2T[0][:, f], w2T[1][:, f]), f == 0, f == FT - 1)
                    mm.then_inc(hidden_used, 1)

            turn_fx(0)
            ranks(TILES - 2)
            turn_xhat(TILES - 1, 1)
            pe.wait_ge(w_split, 1)
            hidden(0)
            logits(TILES - 1)
            turn_fx(1)
            ranks(TILES - 1)
            pe.wait_ge(w_split, 2)
            output(0)
            with pe.Fori(1, BLOCKS - 1) as b:
                hidden(b)
                turn_fx(b + 1)
                output(b)
            hidden(BLOCKS - 1)
            output(BLOCKS - 1)

        @block.scalar
        def _(act):
            a = nc.scalar
            act.dma_start(wnat[:, 0], Wq.rearrange("(k p) d -> p k d", p=P)).then_inc(weights_in, 16)
            act.dma_start(wnat[:, 1], Wk.rearrange("(k p) d -> p k d", p=P)).then_inc(weights_in, 16)
            act.dma_start(wnat[:, 2], WvT.rearrange("(k p) d -> p k d", p=P)).then_inc(weights_in, 16)
            act.dma_start(rwnat, router_wT.rearrange("(k p) e -> p k e", p=P)).then_inc(weights_in, 16)
            act.dma_start(b1_sb[:], b1.rearrange("(f p) -> p f", p=P), allow_slow_non_contiguous=True) \
                .then_inc(biases_in, 16)
            act.dma_start(b2_sb[:], b2.rearrange("(o d) -> o d", o=1).broadcast_to([P, D])).then_inc(biases_in, 16)

            def copy(dst, src):
                return a.activation(dst, src, ACT.Copy)

            def make_mask(n, t):
                act.wait_ge(edges_in, 16 * n + 16)
                at_least(act, scores_taken, CH * (n - 1))
                a.activation(no_edge[:, t], edges_sb[:], ACT.Copy, bias=NO_EDGE, scale=-NO_EDGE) \
                    .then_inc(mask_ready, 1)

            act.wait_ge(weights_in, 16 * 4)
            copy(wvT_hi, wnat[:, 2]).then_inc(a_hi_out, 1)
            copy(rwT_hi[:], rwnat).then_inc(a_hi_out, 1)

            def prep_norm(m):
                i = group_of(m)
                act.wait_ge(shift1_ready, i + 1)
                at_least(act, xn_turned, m - 1)
                a.activation(xhat[:, m % 2], tokens[:, m * D:(m + 1) * D], ACT.Identity,
                             bias=shift1[:, m:m + 1], scale=rstd1[:, m:m + 1]).then_inc(xn_ready, 1)

            def prep_hi(m):
                act.wait_ge(xn_turned, m + 1)
                copy(xnT_hi[:, :, m * P:(m + 1) * P],
                     turn_ps[m % 2][:, 0:KC * P].rearrange("p (k t) -> p k t", k=KC)).then_inc(xn_hi_out, 1)

            def prep_v(m):
                act.wait_ge(v_ready, m + 1)
                copy(v_hi[:, m * VW:m * VW + D], score_ps[m % 2][:, 0:D]).then_inc(v_hi_out, 1)

            prep_norm(0)
            prep_norm(1)
            for m in range(TILES):
                prep_hi(m)
                if m == 0:
                    act.wait_ge(a_ready, 1)
                    copy(a_hi[:], qT_ps).then_inc(a_hi_out, 1)
                if m + 2 < TILES:
                    prep_norm(m + 2)
                if m > 0:
                    prep_v(m - 1)
            prep_v(TILES - 1)
            make_mask(0, 0)
            make_mask(1, 1)

            def queries_hi(n, h, b):
                act.wait_ge(q_ready, b + 1)
                at_least(act, q_split, n)
                at_least(act, scores_ready, CH * (n - 1))
                copy(qT_hi[:, :, h * P:(h + 1) * P], qT_ps[:, :, h * P:(h + 1) * P]).then_inc(q_hi_out, 1)

            def exps(m, t):
                act.wait_ge(minus_max_ready, m + 1)
                for part in (probs[:, t, 0:HEAD], probs[:, t, HEAD:KEYS]):
                    a.activation(part, part, ACT.Exp, bias=minus_max[:, t:t + 1]).then_inc(exp_done, 1)

            def probs_hi(m, t, g):
                act.wait_ge(probs_turned, CH * m + g + 1)
                at_least(act, values_done, CH * m + g - 1)
                s = (CH * t + g) % 2
                copy(probsT_hi[:, s, 0:width(g)], turn_ps[s][:, 0:width(g)]).then_inc(probs_hi_out, 1)

            def router_hi(m):
                act.wait_ge(xhat_turned, m + 1)
                at_least(act, logits_ready, m)
                copy(rT_hi[:], rT_ps).then_inc(router_hi_out, 1)

            def router_exps(m):
                act.wait_ge(best_ready, m + 1)
                at_least(act, gates_ready, m)
                a.activation(router_exp[:], logits_sb[:], ACT.Exp, bias=best[:, 1:2],
                             accum_out=router_sum[:]).then_inc(router_exp_done, 1)

            def step(n, t, next_block=None, old=True, post=True, mask=True):
                if old:
                    exps(n - 1, 1 - t)
                for g in range(CH):
                    if old:
                        probs_hi(n - 1, 1 - t, g)
                    if g == 3 and post:
                        router_hi(n - 2)
                    if g == 2 and next_block is not None:
                        queries_hi(n + 1, 1 - t, next_block)
                    if g == 0 and mask:
                        make_mask(n + 1, 1 - t)
                    if g == CH - 1 and post:
                        router_exps(n - 2)

            queries_hi(0, 0, 0)
            queries_hi(1, 1, 0)
            step(1, 1, next_block=1, post=False)
            step(2, 0, next_block=1)
            with act.Fori(1, BLOCKS - 1) as b:
                step(2 * b + 1, 1, next_block=b + 1)
                step(2 * b + 2, 0, next_block=b + 1)
            step(TILES - 1, 1, mask=False)
            act.wait_ge(w1_in, 16)
            act.wait_ge(scores_ready, CH * TILES)
            copy(w1T[0], w1nat).then_inc(w_hi_out, 1)
            step(TILES, 0, mask=False)
            act.wait_ge(w2_in, 16)
            copy(w2T[0], w2nat).then_inc(w_hi_out, 1)


            def fx_hi(b):
                act.wait_ge(fx_turned, b + 1)
                at_least(act, hidden_ready, FP * b)
                copy(qT_hi[:], qT_ps).then_inc(fx_hi_out, 1)

            def gelu(b, p):
                act.wait_ge(hidden_ready, FP * b + p + 1)
                at_least(act, hidden_split, FP * (b - 1) + p + 1)
                for i in range(2):
                    f = 2 * p + i
                    ins = a.activation(hT[:, f], hidden_ps[p][:, i * B:(i + 1) * B], ACT.Gelu, bias=b1_sb[:, f:f + 1])
                ins.then_inc(gelu_done, 1)

            def hidden_hi(b, p):
                act.wait_ge(gelu_done, FP * b + p + 1)
                at_least(act, hidden_used, FP * (b - 1) + p + 1)
                copy(hT_hi[:, 2 * p:2 * p + 2], hT[:, 2 * p:2 * p + 2]).then_inc(hidden_hi_out, 1)

            def ffn(b, more=True):
                for p in range(FP + 1):
                    if p < FP:
                        gelu(b, p)
                    if p > 0:
                        hidden_hi(b, p - 1)
                if more:
                    fx_hi(b + 1)

            fx_hi(0)
            router_hi(TILES - 1)
            router_exps(TILES - 1)
            act.wait_ge(biases_in, 16 * 2)
            ffn(0)
            with act.Fori(1, BLOCKS - 1) as b:
                ffn(b)
            ffn(BLOCKS - 1, more=False)

        @block.vector
        def _(dve):
            v = nc.vector

            def lo(dst, src, hi):
                return v.tensor_tensor(dst, src, hi, ALU.subtract)

            ones_col = v_hi[:].rearrange("p (t w) -> p t w", t=TILES)[:, :, D:D + 1]
            zero_col = v_hi[:].rearrange("p (t w) -> p t w", t=TILES)[:, :, D + 1:D + 2]
            v.memset(ones_col.bitcast(F32), 1.0).then_inc(v_columns_made, 1)
            v.memset(zero_col.bitcast(F32), 0.0).then_inc(v_columns_made, 1)
            v.memset(queue[:], 0.0).then_inc(gate_seq, 1)
            st = stats[:].rearrange("p (t s) -> p t s", t=TILES)

            def statistics(m):
                if m in [first_tile for first_tile, _ in GROUPS]:
                    dve.wait_ge(x_in[group_of(m)], 16)
                v.bn_stats(st[:, m], tokens[:, m * D:(m + 1) * D]).then_inc(stats_made, 1)

            def group_variance(i):
                first_tile, end = GROUPS[i]
                dve.wait_ge(stats_made, end)
                c = slice(first_tile, end)
                even_mean, even_var, odd_mean, odd_var = st[:, c, 1], st[:, c, 2], st[:, c, 4], st[:, c, 5]
                v.tensor_tensor(mean1[:, c], even_mean, odd_mean, ALU.add).then_inc(ln_seq, 1)
                v.tensor_tensor(tmp1[:, c], even_mean, odd_mean, ALU.subtract).then_inc(ln_seq, 1)
                v.tensor_tensor(tmp2[:, c], even_var, odd_var, ALU.add).then_inc(ln_seq, 1)
                dve.wait_ge(ln_seq, 5 * i + 3)
                v.scalar_tensor_tensor(out=tmp1[:, c], in0=tmp1[:, c], scalar=0.25, in1=tmp1[:, c], op0=ALU.mult,
                                       op1=ALU.mult).then_inc(ln_seq, 1)
                v.tensor_scalar(tmp2[:, c], tmp2[:, c], 1.0 / D, EPS, ALU.mult, ALU.add).then_inc(ln_seq, 1)
                dve.wait_ge(ln_seq, 5 * i + 5)
                v.tensor_tensor(rstd1[:, c], tmp1[:, c], tmp2[:, c], ALU.add).then_inc(var1_ready, 1)

            def group_shift(i):
                c = slice(*GROUPS[i])
                dve.wait_ge(rstd1_ready, i + 1)
                v.scalar_tensor_tensor(out=shift1[:, c], in0=mean1[:, c], scalar=-0.5, in1=rstd1[:, c], op0=ALU.mult,
                                       op1=ALU.mult).then_inc(shift1_ready, 1)

            def normalise(dst, m, mean, rstd):
                return v.tensor_scalar(dst, tokens[:, tile_of(m)], mean[:, ds(m, 1)], rstd[:, ds(m, 1)],
                                       ALU.subtract, ALU.mult)

            def prep_lo(m):
                dve.wait_ge(xn_hi_out, m + 1)
                tile = slice(m * P, (m + 1) * P)
                lo(xnT_lo[:, :, tile], turn_ps[m % 2][:, 0:KC * P].rearrange("p (k t) -> p k t", k=KC),
                   xnT_hi[:, :, tile]).then_inc(xn_split, 1)

            def prep_v(m):
                dve.wait_ge(v_hi_out, m + 1)
                cols = slice(m * VW, m * VW + D)
                lo(v_lo[:, cols], score_ps[m % 2][:, 0:D], v_hi[:, cols]).then_inc(v_split, 1)

            def statistics_ahead(m):
                statistics(m)
                if m + 1 == GROUPS[group_of(m)][1]:
                    group_variance(group_of(m))

            AHEAD = 8
            for m in range(2):
                statistics_ahead(m)
            dve.wait_ge(a_hi_out, 2)
            lo(wvT_lo, wnat[:, 2], wvT_hi).then_inc(a_split, 1)
            lo(rwT_lo[:], rwnat, rwT_hi[:]).then_inc(a_split, 1)
            group_shift(0)
            for m in range(2, AHEAD):
                statistics_ahead(m)
                if m == 6:
                    group_shift(1)
            for m in range(TILES):
                if m > 0 and m + 3 in [first_tile for first_tile, _ in GROUPS[2:]]:
                    group_shift(group_of(m + 3))
                prep_lo(m)
                if m == 1:
                    dve.wait_ge(a_hi_out, 3)
                    lo(a_lo[:], qT_ps, a_hi[:]).then_inc(a_split, 1)
                if m + AHEAD < TILES:
                    statistics_ahead(m + AHEAD)
                if m > 0:
                    prep_v(m - 1)
            prep_v(TILES - 1)

            def queries_lo(n, h):
                dve.wait_ge(q_hi_out, n + 1)
                cols = slice(h * P, (h + 1) * P)
                lo(qT_lo[:, :, cols], qT_ps[:, :, cols], qT_hi[:, :, cols]).then_inc(q_split, 1)

            def take_scores(n, t, g):
                if g == 0:
                    at_least(dve, probs_turned, CH * (n - 1))
                    dve.wait_ge(mask_ready, n + 1)
                wait_apart(dve, scores_ready, CH * n + g + 1)
                w = width(g)
                keys = slice(g * CHUNK, g * CHUNK + w)
                v.tensor_tensor_reduce(probs[:, t, keys], score_ps[(CH * t + g) % 2][:, 0:w], no_edge[:, t, keys],
                                       1.0, -BIG, ALU.add, ALU.max, chunk_max[:, t, g:g + 1]) \
                    .then_inc(scores_taken, 1)

            def maximum(n, t):
                dve.wait_ge(scores_taken, CH * (n + 1))
                v.tensor_reduce(row_max[:, t:t + 1], chunk_max[:, t], AX.X, ALU.max).then_inc(max_seq, 1)
                dve.wait_ge(max_seq, n + 1)
                v.tensor_scalar(minus_max[:, t:t + 1], row_max[:, t:t + 1], -1.0, None, ALU.mult) \
                    .then_inc(minus_max_ready, 1)
                v.tensor_scalar(has_edge[:, t:t + 1], row_max[:, t:t + 1], NO_EDGE / 2, None, ALU.is_gt)

            def probs_lo(m, t, g):
                dve.wait_ge(probs_hi_out, CH * m + g + 1)
                s = (CH * t + g) % 2
                w = width(g)
                lo(probsT_lo[:, s, 0:w], turn_ps[s][:, 0:w], probsT_hi[:, s, 0:w]).then_inc(probs_split, 1)

            def finish(m, t):
                seq = FINISH_STEPS * m

                def link(ins, k):
                    ins.then_inc(finish_seq, 1)
                    dve.wait_ge(finish_seq, seq + k)

                dve.wait_ge(values_done, CH * (m + 1))
                link(v.reciprocal(inv_sum[:, t:t + 1], attn_ps[t][:, D:D + 1]), 1)
                link(v.tensor_tensor(row_scale[:, t:t + 1], inv_sum[:, t:t + 1], has_edge[:, t:t + 1], ALU.mult), 2)
                v.scalar_tensor_tensor(out=tokens[:, tile_of(m)], in0=attn_ps[t][:, 0:D], scalar=row_scale[:, t:t + 1],
                                       in1=tokens[:, tile_of(m)], op0=ALU.mult, op1=ALU.add).then_inc(attn_taken, 1)
                wait_apart(dve, attn_taken, m + 1)
                link(v.bn_stats(stats2[:], tokens[:, tile_of(m)]), 3)
                dve.sem_inc(waited_apart, 1)
                link(v.bn_aggr(meanvar2[:], stats2[:]), 4)
                at_least(dve, rstd2_ready, m)
                v.tensor_scalar(var_eps[:], meanvar2[:, 1:2], EPS, None, ALU.add).then_inc(var2_ready, 1)
                link(v.tensor_copy(mean2[:, ds(m, 1)], meanvar2[:, 0:1]), 5)

            def second_norm(m, t):
                dve.wait_ge(rstd2_ready, m + 1)
                dve.wait_ge(finish_seq, FINISH_STEPS * (m + 1))
                at_least(dve, xhat_turned, m - 1)
                normalise(xhat[:, t], m, mean2, rstd2).then_inc(xhat_ready, 1)

            def router_lo(m):
                dve.wait_ge(router_hi_out, m + 1)
                lo(rT_lo[:], rT_ps, rT_hi[:]).then_inc(router_split, 1)

            def route_link(m, ins, k):
                ins.then_inc(route_seq, 1)
                dve.wait_ge(route_seq, ROUTE_STEPS * m + k)

            def pick(m):
                dve.wait_ge(logits_ready, m + 1)
                at_least(dve, router_exp_done, m)
                route_link(m, v.tensor_copy(logits_sb[:], logits_ps), 1)
                route_link(m, v.tensor_reduce(best[:, 0:1], logits_sb[:], AX.X, ALU.max), 2)
                v.tensor_scalar(best[:, 1:2], best[:, 0:1], -1.0, None, ALU.mult).then_inc(best_ready, 1)
                route_link(m, v.scalar_tensor_tensor(out=cand[:], in0=logits_sb[:], scalar=best[:, 0:1], in1=rev[:],
                                                     op0=ALU.is_equal, op1=ALU.mult), 3)
                route_link(m, v.tensor_reduce(best[:, 2:3], cand[:], AX.X, ALU.max), 4)
                route_link(m, v.tensor_scalar(first[:], rev[:], best[:, 2:3], None, ALU.is_equal), 5)
                route_link(m, v.scalar_tensor_tensor(out=rest[:], in0=first[:], scalar=-BIG, in1=logits_sb[:],
                                                     op0=ALU.mult, op1=ALU.add), 6)
                route_link(m, v.tensor_reduce(best[:, 3:4], rest[:], AX.X, ALU.max), 7)
                route_link(m, v.scalar_tensor_tensor(out=cand[:], in0=rest[:], scalar=best[:, 3:4], in1=rev[:],
                                                     op0=ALU.is_equal, op1=ALU.mult), 8)
                route_link(m, v.tensor_reduce(best[:, 4:5], cand[:], AX.X, ALU.max), 9)
                at_least(dve, ranks_ready, m)
                v.scalar_tensor_tensor(out=picked[:], in0=rev[:], scalar=best[:, 4:5], in1=first[:],
                                       op0=ALU.is_equal, op1=ALU.add).then_inc(picks_ready, 1)

            def gate(m):
                seq = 1 + GATE_STEPS * m
                dve.wait_ge(ranks_ready, m + 1)
                dve.wait_ge(router_exp_done, m + 1)
                v.tensor_tensor(rank[:], rank_ps, queue[:], ALU.add).then_inc(gate_seq, 1)
                v.reciprocal(best[:, 5:6], router_sum[:])
                dve.wait_ge(gate_seq, seq + 1)
                v.tensor_tensor(queue[:], total_ps, queue[:], ALU.add)
                v.scalar_tensor_tensor(out=kept[:], in0=rank[:], scalar=float(CAPACITY), in1=picked[:],
                                       op0=ALU.is_lt, op1=ALU.mult).then_inc(gate_seq, 1)
                dve.wait_ge(gate_seq, seq + 2)
                v.tensor_tensor_reduce(cand[:], kept[:], router_exp[:], 1.0, 0.0, ALU.mult, ALU.add,
                                       best[:, 6:7]).then_inc(gate_seq, 1)
                dve.wait_ge(gate_seq, seq + 3)
                v.tensor_tensor(gates[:, ds(m, 1)], best[:, 6:7], best[:, 5:6], ALU.mult).then_inc(gates_ready, 1)

            def step(n, t, next_block=None, new=True, old=True, post=True, late=True):
                m, u = n - 1, 1 - t
                for g in range(CH + 1):
                    if new and g < CH:
                        take_scores(n, t, g)
                    if old and 1 <= g:
                        probs_lo(m, u, g - 1)
                    if new and g == CH - 1:
                        maximum(n, t)
                    if post and g == 1:
                        finish(n - 2, t)
                    if late and g == 2:
                        gate(n - 3)
                    if post and g == 3:
                        second_norm(n - 2, t)
                    if post and g == 4:
                        router_lo(n - 2)
                    if g == 5 and next_block is not None:
                        queries_lo(n + 1, u)
                    if post and g == CH:
                        pick(n - 2)

            queries_lo(0, 0)
            queries_lo(1, 1)
            step(0, 0, old=False, post=False, late=False)
            step(1, 1, next_block=1, post=False, late=False)
            step(2, 0, next_block=1, late=False)
            with dve.Fori(1, BLOCKS - 1) as b:
                step(2 * b + 1, 1, next_block=b + 1)
                step(2 * b + 2, 0, next_block=b + 1)
            step(TILES - 1, 1)
            dve.wait_ge(w_hi_out, 1)
            lo(w1T[1], w1nat, w1T[0]).then_inc(w_split, 1)
            step(TILES, 0, new=False)
            dve.wait_ge(w_hi_out, 2)
            lo(w2T[1], w2nat, w2T[0]).then_inc(w_split, 1)

            def fx_norm(b):
                at_least(dve, fx_turned, b)
                normalise(fx[:, 0], 2 * b, mean2, rstd2)
                normalise(fx[:, 1], 2 * b + 1, mean2, rstd2).then_inc(fx_ready, 1)

            def fx_lo(b):
                dve.wait_ge(fx_hi_out, b + 1)
                lo(qT_lo[:], qT_ps, qT_hi[:]).then_inc(fx_split, 1)

            def ffn(b, more=True):
                if more and not (isinstance(b, int) and b == 0):
                    fx_norm(b + 1)
                for p in range(FP):
                    dve.wait_ge(hidden_hi_out, FP * b + p + 1)
                    pair = slice(2 * p, 2 * p + 2)
                    lo(hT_lo[:, pair], hT[:, pair], hT_hi[:, pair]).then_inc(hidden_split, 1)
                if more:
                    fx_lo(b + 1)
                dve.wait_ge(hidden_used, FP * (b + 1))
                for t in range(2):
                    v.tensor_tensor(y_sb[:, t], y_ps[t][:, 0:D], b2_sb[:], ALU.add).then_inc(y_taken, 1)
                for t in range(2):
                    m = 2 * b + t
                    dve.wait_ge(y_taken, m + 1)
                    v.scalar_tensor_tensor(out=tokens[:, tile_of(m)], in0=y_sb[:, t], scalar=gates[:, ds(m, 1)],
                                           in1=tokens[:, tile_of(m)], op0=ALU.mult, op1=ALU.add) \
                        .then_inc(out_ready, 1)

            fx_norm(0)
            fx_lo(0)
            finish(TILES - 1, 1)
            gate(TILES - 2)
            second_norm(TILES - 1, 1)
            router_lo(TILES - 1)
            fx_norm(1)
            pick(TILES - 1)
            gate(TILES - 1)
            dve.wait_ge(gates_ready, TILES)
            dve.wait_ge(biases_in, 16 * 2)
            ffn(0)
            with dve.Fori(1, BLOCKS - 1) as b:
                ffn(b)
            ffn(BLOCKS - 1, more=False)


def kernel(**inputs):
    import numpy as _np
    import concourse.bacc as _bacc
    from concourse import mybir as _mybir
    from concourse.bass_utils import run_bass_kernel_spmd as _run

    n, d = inputs["x"].shape
    pad = -n % P
    laid_out = {
        "x": _np.pad(inputs["x"], ((0, pad), (0, 0))),
        "edges": _np.pad(_np.asarray(inputs["adj"]).T, ((0, pad), (0, pad))),
        "wq": inputs["L0_gnn_Wq"],
        "wk": inputs["L0_gnn_Wk"],
        "wvT": _np.asarray(inputs["L0_gnn_Wv"]).T,
        "router_wT": _np.asarray(inputs["L0_ffn_router_w"]).T,
        "w1T": _np.asarray(inputs["L0_ffn_w1"]).T,
        "b1": inputs["L0_ffn_b1"],
        "w2T": _np.asarray(inputs["L0_ffn_w2"]).T,
        "b2": inputs["L0_ffn_b2"],
    }
    nc = _bacc.Bacc("TRN2", target_bir_lowering=False, num_devices=1)
    arrays, args = {}, []
    for name, array in laid_out.items():
        a = _np.ascontiguousarray(array)
        arrays[f"in_{name}"] = a
        args.append(nc.dram_tensor(f"in_{name}", a.shape, _mybir.dt.from_np(a.dtype), kind="ExternalInput").ap())
    args.append(nc.dram_tensor("out", (n + pad, d), _mybir.dt.float32, kind="ExternalOutput").ap())
    build(nc, *args)
    r = _run(nc, [arrays], core_ids=[0])
    return r.results[0]["out"][:n]
```

```python
from contextlib import ExitStack

import concourse.bass as bass
from concourse import mybir

ACT = mybir.ActivationFunctionType
ALU = mybir.AluOpType
AX = mybir.AxisListType
F32 = mybir.dt.float32
F32R = mybir.dt.float32r
BF16 = mybir.dt.bfloat16
U8 = mybir.dt.uint8

P = 128
EPS = 1e-5
CAPACITY = 256
NO_EDGE = -1e30
BIG = 3e38


def ds(start, size):
    return bass.ds(start, size)


def at_least(engine, semaphore, value):
    if not isinstance(value, int) or value > 0:
        engine.wait_ge(semaphore, value)


def build(nc, x, edges, Wq, Wk, WvT, router_wT, w1T_in, b1, w2T_in, b2, out):
    N, D = x.shape
    E = router_wT.shape[1]
    F = w1T_in.shape[1]
    TILES = N // P
    BLOCKS = TILES // 2
    KEYS = TILES * P
    KC = D // P
    B = 2 * P
    CHUNK = 512
    CH = (KEYS + CHUNK - 1) // CHUNK
    FT = F // P
    FP = FT // 2
    VW = D + 2
    HEAD = 2 * CHUNK
    assert TILES == 2 * BLOCKS and BLOCKS > 4 and D == 256 and F % B == 0 and CH == 7
    assert KC * P + 4 * E == CHUNK

    def width(g):
        return min(CHUNK, KEYS - g * CHUNK)

    with ExitStack() as ctx:
        def sb(name, shape, dt):
            return ctx.enter_context(nc.sbuf_tensor(name, shape, dt))

        def sem(name):
            return ctx.enter_context(nc.semaphore(name))

        GROUPS = [(0, 2)] + [(m, m + 4) for m in range(2, TILES, 4)]

        tokens = sb("tokens", [P, TILES * D], F32)
        xnT_hi = sb("xnT_hi", [P, KC, KEYS], F32R)
        xnT_lo = sb("xnT_lo", [P, KC, KEYS], F32R)
        v_hi = sb("v_hi", [P, TILES * VW], F32R)
        v_lo = sb("v_lo", [P, TILES * VW], F32R)
        probs = sb("probs", [P, 2, KEYS], F32)
        probsT_hi = sb("probsT_hi", [P, 2, CHUNK], F32R)
        probsT_lo = sb("probsT_lo", [P, 2, CHUNK], F32R)
        edges_sb = sb("edges_sb", [P, KEYS], U8)
        no_edge = sb("no_edge", [P, 2, KEYS], BF16)
        qT_hi = sb("qT_hi", [P, KC, B], F32R)
        qT_lo = sb("qT_lo", [P, KC, B], F32R)
        a_hi = sb("a_hi", [P, KC, D], F32R)
        a_lo = sb("a_lo", [P, KC, D], F32R)
        xhat = sb("xhat", [P, 2, D], F32)
        rT_hi = sb("rT_hi", [P, KC, P], F32R)
        rT_lo = sb("rT_lo", [P, KC, P], F32R)
        rwT = sb("rwT", [P, KC, 2 * E], F32R)
        ident = sb("ident", [P, P], F32)
        before = sb("before", [P, P], BF16)
        ones = sb("ones", [P, P], BF16)
        rev = sb("rev", [P, E], F32)
        minus_half = sb("minus_half", [P, TILES], F32)
        stats = sb("stats", [P, TILES * 6], F32)
        mean1 = sb("mean1", [P, TILES], F32)
        rstd1 = sb("rstd1", [P, TILES], F32)
        mean2 = sb("mean2", [P, TILES], F32)
        rstd2 = sb("rstd2", [P, TILES], F32)
        gates = sb("gates", [P, TILES], F32)
        tmp1 = sb("tmp1", [P, TILES], F32)
        tmp2 = sb("tmp2", [P, TILES], F32)
        shift1 = sb("shift1", [P, TILES], F32)
        chunk_max = sb("chunk_max", [P, 2, CH], F32)
        row_max = sb("row_max", [P, 2], F32)
        minus_max = sb("minus_max", [P, 2], F32)
        has_edge = sb("has_edge", [P, 2], F32)
        inv_sum = sb("inv_sum", [P, 2], F32)
        row_scale = sb("row_scale", [P, 2], F32)
        stats2 = sb("stats2", [P, 6], F32)
        meanvar2 = sb("meanvar2", [P, 2], F32)
        var_eps = sb("var_eps", [P, 1], F32)
        best = sb("best", [P, 8], F32)
        cand = sb("cand", [P, E], F32)
        first = sb("first", [P, E], F32)
        rest = sb("rest", [P, E], F32)
        picked = sb("picked", [P, E], BF16)
        logits_sb = sb("logits_sb", [P, E], F32)
        router_exp = sb("router_exp", [P, E], F32)
        router_sum = sb("router_sum", [P, 1], F32)
        rank = sb("rank", [P, E], F32)
        kept = sb("kept", [P, E], F32)
        queue = sb("queue", [P, E], F32)
        b1_sb = sb("b1_sb", [P, FT], F32)
        b2_sb = sb("b2_sb", [P, D], F32)

        wnat = probs[:, 0, 0:3 * KC * D].rearrange("p (w k d) -> p w k d", w=3, k=KC)
        rwnat = probs[:, 1, 0:KC * E].rearrange("p (k e) -> p k e", k=KC)
        second_edges = probs[:, 1, KEYS - KEYS // 4:KEYS].bitcast(U8)
        wvT_hi = probsT_hi[:, 0, :].rearrange("p (k d) -> p k d", k=KC)
        wvT_lo = probsT_lo[:, 0, :].rearrange("p (k d) -> p k d", k=KC)
        xn_ring = [probs[:, 1, (i + 1) * D:(i + 2) * D] for i in range(4)]
        w1nat = probs[:, 0, 0:KC * F].rearrange("p (k f) -> p k f", k=KC)
        w2nat = no_edge[:].rearrange("p a k -> p (a k)")[:, 0:2 * FT * D].bitcast(F32) \
            .rearrange("p (f d) -> p f d", f=FT)
        w1T = [s[:, 0, 0:KC * F].rearrange("p (k f) -> p k f", k=KC) for s in (xnT_hi, xnT_lo)]
        w2T = [s[:, 1, 0:FT * D].rearrange("p (f d) -> p f d", f=FT) for s in (xnT_hi, xnT_lo)]
        hT = probs[:, 1, 0:FT * B].rearrange("p (f b) -> p f b", f=FT)
        hT_hi = v_hi[:, 0:FT * B].rearrange("p (f b) -> p f b", f=FT)
        hT_lo = v_lo[:, 0:FT * B].rearrange("p (f b) -> p f b", f=FT)
        fx = probs[:, 0, KC * F:KC * F + 2 * D].rearrange("p (t d) -> p t d", t=2)
        y_sb = probs[:, 0, KC * F + 2 * D:KC * F + 4 * D].rearrange("p (t d) -> p t d", t=2)

        def bank(name):
            return ctx.enter_context(nc.psum_tensor(name, [P, CHUNK], F32))

        score_ps = [bank(f"score_ps{i}") for i in range(2)]
        turn_ps = [bank(f"turn_ps{i}") for i in range(2)]
        attn_ps = [bank(f"attn_ps{i}") for i in range(2)]
        q_ps = bank("q_ps")
        route_ps = bank("route_ps")
        qT_ps = q_ps[:].rearrange("p (k b) -> p k b", k=KC)
        rT_ps = route_ps[:, 0:KC * P].rearrange("p (k t) -> p k t", k=KC)
        at = KC * P
        logits_ps = route_ps[:, at:at + E]
        logits2_ps = route_ps[:, at:at + 2 * E]
        rank_ps = route_ps[:, at + 2 * E:at + 3 * E]
        total_ps = route_ps[:, at + 3 * E:at + 4 * E]
        prep_ps = [*turn_ps, route_ps]
        v_ps = [(*attn_ps, score_ps[1] if m < 8 else q_ps)[m % 3] for m in range(TILES)]
        hidden_ps = [*score_ps, *turn_ps]
        y_ps = attn_ps

        wqk_in = sem("wqk_in")
        wv_in = sem("wv_in")
        rw_in = sem("rw_in")
        biases_in = sem("biases_in")
        x_in = [sem(f"x_in{i}") for i in range(len(GROUPS))]
        edges_in = sem("edges_in")
        second_edges_in = sem("second_edges_in")
        consts_made = sem("consts_made")
        zeroed = sem("zeroed")
        v_columns_made = sem("v_columns_made")
        a_ready = sem("a_ready")
        a_hi_out = sem("a_hi_out")
        a_split = sem("a_split")
        wv_hi_out = sem("wv_hi_out")
        wv_split = sem("wv_split")
        rw_hi_out = sem("rw_hi_out")
        rw_split = sem("rw_split")
        stats_made = sem("stats_made")
        ln_seq = sem("ln_seq")
        xn_ready = sem("xn_ready")
        xn_turned = sem("xn_turned")
        xn_hi_out = sem("xn_hi_out")
        xn_split = sem("xn_split")
        norm1_ready = sem("norm1_ready")
        v_ready = sem("v_ready")
        v_hi_out = sem("v_hi_out")
        v_split = sem("v_split")
        q_ready = sem("q_ready")
        q_hi_out = sem("q_hi_out")
        q_split = sem("q_split")
        first_mask_ready = sem("first_mask_ready")
        second_mask_ready = sem("second_mask_ready")
        mask_ready = sem("mask_ready")
        scores_ready = sem("scores_ready")
        scores_taken = sem("scores_taken")
        max_seq = sem("max_seq")
        minus_max_ready = sem("minus_max_ready")
        exp_done = sem("exp_done")
        probs_turned = sem("probs_turned")
        probs_hi_out = sem("probs_hi_out")
        probs_split = sem("probs_split")
        values_done = sem("values_done")
        attn_taken = sem("attn_taken")
        finish_seq = sem("finish_seq")
        var2_ready = sem("var2_ready")
        rstd2_ready = sem("rstd2_ready")
        xhat_ready = sem("xhat_ready")
        xhat_turned = sem("xhat_turned")
        router_hi_out = sem("router_hi_out")
        router_split = sem("router_split")
        logits_ready = sem("logits_ready")
        route_seq = sem("route_seq")
        best_ready = sem("best_ready")
        router_exp_done = sem("router_exp_done")
        picks_ready = sem("picks_ready")
        ranks_ready = sem("ranks_ready")
        gate_seq = sem("gate_seq")
        gates_ready = sem("gates_ready")
        w1_in = sem("w1_in")
        w2_in = sem("w2_in")
        w1_hi_out = sem("w1_hi_out")
        w1_split = sem("w1_split")
        w2_hi_out = sem("w2_hi_out")
        w2_split = sem("w2_split")
        fx_ready = sem("fx_ready")
        fx_turned = sem("fx_turned")
        fx_hi_out = sem("fx_hi_out")
        fx_split = sem("fx_split")
        hidden_ready = sem("hidden_ready")
        gelu_done = sem("gelu_done")
        hidden_hi_out = sem("hidden_hi_out")
        hidden_split = sem("hidden_split")
        hidden_used = sem("hidden_used")
        y_taken = sem("y_taken")
        out_ready = sem("out_ready")
        stored = sem("stored")
        waited_apart = sem("waited_apart")

        AT_PACE = [[g] for g in range(CH)] + [[], []]
        AHEAD_OF_PACE = [[0, 1], [2], [3, 4], [5, 6], [], [], [], [], []]
        LAST_EXPS = (4, 5)

        FINISH_STEPS, ROUTE_STEPS, GATE_STEPS = 5, 9, 3
        block = ctx.enter_context(nc.Block())

        def group_of(m):
            return next(i for i, (first_tile, end) in enumerate(GROUPS) if m < end)

        def wait_apart(engine, semaphore, value):
            at_least(engine, semaphore, value)
            engine.sem_inc(waited_apart, 1)

        def tile_of(m):
            return ds(m * D, D)

        @block.sync
        def _(sp):
            def load_x(i):
                first_tile, end = GROUPS[i]
                sp.dma_start(tokens[:, first_tile * D:end * D].rearrange("p (t d) -> p t d", d=D),
                             x[first_tile * P:end * P].rearrange("(t p) d -> p t d", p=P)).then_inc(x_in[i], 16)

            load_x(0)
            load_x(1)
            sp.dma_start(wnat[:, 2], WvT.rearrange("(k p) d -> p k d", p=P)).then_inc(wv_in, 16)
            load_x(2)
            sp.dma_start(edges_sb[:], edges[0:P]).then_inc(edges_in, 16)
            load_x(3)
            sp.dma_start(second_edges, edges[P:2 * P]).then_inc(second_edges_in, 16)
            for i in range(4, len(GROUPS)):
                load_x(i)
            sp.dma_start(b1_sb[:], b1.rearrange("(f p) -> p f", p=P), allow_slow_non_contiguous=True) \
                .then_inc(biases_in, 16)
            sp.dma_start(b2_sb[:], b2.rearrange("(o d) -> o d", o=1).broadcast_to([P, D])).then_inc(biases_in, 16)

            def load_edges(n):
                sp.dma_start(edges_sb[:], edges[ds(n * P, P)]).then_inc(edges_in, 16)

            sp.wait_ge(first_mask_ready, CH)
            load_edges(2)
            with sp.Fori(3, TILES) as n:
                wait_apart(sp, mask_ready, n - 2)
                load_edges(n)

            sp.wait_ge(scores_taken, CH * TILES)
            sp.dma_start(w2nat, w2T_in.rearrange("(f p) d -> p f d", p=P)).then_inc(w2_in, 16)
            sp.wait_ge(probs_turned, CH * (TILES - 1))
            sp.dma_start(w1nat, w1T_in.rearrange("(k p) f -> p k f", p=P)).then_inc(w1_in, 16)

            with sp.Fori(0, BLOCKS - 1) as b:
                wait_apart(sp, out_ready, 2 * b + 2)
                sp.dma_start(out[ds(b * B, B)].rearrange("(t p) d -> p t d", p=P),
                             tokens[:, ds(b * 2 * D, 2 * D)].rearrange("p (t d) -> p t d", t=2)) \
                    .then_inc(stored, 16)
            for m in (TILES - 2, TILES - 1):
                sp.wait_ge(out_ready, m + 1)
                sp.dma_start(out[m * P:(m + 1) * P], tokens[:, m * D:(m + 1) * D]).then_inc(stored, 16)
            sp.wait_ge(stored, 16 * (BLOCKS + 1))

        @block.gpsimd
        def _(pool):
            g = nc.gpsimd
            g.memset(ident[:], 0.0).then_inc(zeroed, 1)
            g.memset(before[:], 0.0).then_inc(zeroed, 1)
            g.memset(ones[:], 1.0).then_inc(consts_made, 1)
            g.memset(minus_half[:], -0.5).then_inc(consts_made, 1)
            pool.wait_ge(zeroed, 2)
            g.affine_select(out=ident[:], in_=ident[:], compare_op=ALU.not_equal, fill=1.0, base=0,
                            pattern=[[-1, P]], channel_multiplier=1).then_inc(consts_made, 1)
            g.affine_select(out=before[:], in_=before[:], compare_op=ALU.is_ge, fill=1.0, base=0,
                            pattern=[[-1, P]], channel_multiplier=1).then_inc(consts_made, 1)
            g.iota(rev[:], pattern=[[-1, E]], base=E, channel_multiplier=0,
                   allow_small_or_imprecise_dtypes=True).then_inc(consts_made, 1)

            pool.wait_ge(consts_made, 5)

            st = stats[:].rearrange("p (t s) -> p t s", t=TILES)

            def group_norm(i):
                first_tile, end = GROUPS[i]
                pool.wait_ge(stats_made, end)
                c = slice(first_tile, end)
                even_mean, even_var, odd_mean, odd_var = st[:, c, 1], st[:, c, 2], st[:, c, 4], st[:, c, 5]
                g.tensor_tensor(tmp1[:, c], even_mean, odd_mean, ALU.subtract).then_inc(ln_seq, 1)
                g.tensor_tensor(tmp2[:, c], even_var, odd_var, ALU.add).then_inc(ln_seq, 1)
                g.tensor_tensor(mean1[:, c], even_mean, odd_mean, ALU.add).then_inc(ln_seq, 1)
                pool.wait_ge(ln_seq, 8 * i + 3)
                g.tensor_tensor(tmp1[:, c], tmp1[:, c], tmp1[:, c], ALU.mult).then_inc(ln_seq, 1)
                g.tensor_scalar(tmp2[:, c], tmp2[:, c], 4.0 / D, 4 * EPS, ALU.mult, ALU.add).then_inc(ln_seq, 1)
                g.tensor_scalar(mean1[:, c], mean1[:, c], -1.0, None, ALU.mult).then_inc(ln_seq, 1)
                pool.wait_ge(ln_seq, 8 * i + 6)
                g.tensor_tensor(tmp1[:, c], tmp1[:, c], tmp2[:, c], ALU.add).then_inc(ln_seq, 1)
                pool.wait_ge(ln_seq, 8 * i + 7)
                g.tensor_tensor(tmp2[:, c], tmp1[:, c], minus_half[:, c], ALU.pow).then_inc(ln_seq, 1)
                pool.wait_ge(ln_seq, 8 * i + 8)
                g.tensor_scalar(rstd1[:, c], tmp2[:, c], 2.0, None, ALU.mult).then_inc(norm1_ready, 1)
                g.tensor_tensor(shift1[:, c], mean1[:, c], tmp2[:, c], ALU.mult).then_inc(norm1_ready, 1)

            def second_mask(chunk):
                pool.wait_ge(second_edges_in, 16)
                keys = slice(chunk * CHUNK, chunk * CHUNK + width(chunk))
                g.tensor_scalar(no_edge[:, 1, keys], second_edges[:, keys], -NO_EDGE, NO_EDGE, ALU.mult, ALU.add) \
                    .then_inc(second_mask_ready, 1)

            for i in range(len(GROUPS)):
                group_norm(i)
                if i >= 2:
                    second_mask(i - 2)
            for i in range(len(GROUPS) - 2, CH):
                second_mask(i)

            def second_power(m):
                pool.wait_ge(var2_ready, m + 1)
                g.tensor_tensor(rstd2[:, ds(m, 1)], var_eps[:], minus_half[:, 0:1], ALU.pow) \
                    .then_inc(rstd2_ready, 1)

            with pool.Fori(0, TILES - 1) as m:
                second_power(m)

            for p in range(FP):
                pool.wait_ge(w2_hi_out, p + 1)
                pair = slice(2 * p, 2 * p + 2)
                g.tensor_tensor(w2T[1][:, pair], w2nat[:, pair], w2T[0][:, pair], ALU.subtract).then_inc(w2_split, 1)
            for p in range(FP):
                pool.wait_ge(w1_hi_out, p + 1)
                pair = slice(p * B, (p + 1) * B)
                g.tensor_tensor(w1T[1][:, :, pair], w1nat[:, :, pair], w1T[0][:, :, pair], ALU.subtract) \
                    .then_inc(w1_split, 1)
            second_power(TILES - 1)

        @block.tensor
        def _(pe):
            def split_product(out_ps, lhs, rhs, start, stop):
                pe.matmul(out_ps, lhs[0], rhs[0], start=start, stop=False)
                pe.matmul(out_ps, lhs[0], rhs[1], start=False, stop=False)
                return pe.matmul(out_ps, lhs[1], rhs[0], start=False, stop=stop)

            def prep_turn(m):
                pe.wait_ge(xn_ready, m + 1)
                at_least(pe, xn_split, m - len(prep_ps) + 1)
                for k in range(KC):
                    mm = pe.transpose(prep_ps[m % len(prep_ps)][:, k * P:(k + 1) * P],
                                      xn_ring[m % len(xn_ring)][:, k * P:(k + 1) * P], ident[:])
                mm.then_inc(xn_turned, 1)

            def prep_v(m):
                pe.wait_ge(xn_split, m + 1)
                at_least(pe, v_split, 1 + max([i for i in range(m) if v_ps[i] is v_ps[m]], default=-1))
                if v_ps[m] is q_ps:
                    pe.wait_ge(q_split, 2)
                for k in range(KC):
                    tile = slice(m * P, (m + 1) * P)
                    mm = split_product(v_ps[m][:, 0:D], (xnT_hi[:, k, tile], xnT_lo[:, k, tile]),
                                       (wvT_hi[:, k], wvT_lo[:, k]), k == 0, k == KC - 1)
                mm.then_inc(v_ready, 1)

            def queries(b):
                at_least(pe, q_split, 2 * b)
                for m in range(KC):
                    for k in range(KC):
                        cols = ds(b * B, B)
                        mm = split_product(qT_ps[:, m], (a_hi[:, k, m * P:(m + 1) * P], a_lo[:, k, m * P:(m + 1) * P]),
                                           (xnT_hi[:, k, cols], xnT_lo[:, k, cols]), k == 0, k == KC - 1)
                mm.then_inc(q_ready, 1)

            def scores(n, t, g):
                if g == 0:
                    pe.wait_ge(q_split, n + 1)
                at_least(pe, scores_taken, CH * n + g - 1)
                ps = score_ps[(CH * t + g) % 2]
                w = width(g)
                for k in range(KC):
                    q = (qT_hi[:, k, t * P:(t + 1) * P], qT_lo[:, k, t * P:(t + 1) * P])
                    keys = slice(g * CHUNK, g * CHUNK + w)
                    mm = split_product(ps[:, 0:w], q, (xnT_hi[:, k, keys], xnT_lo[:, k, keys]), k == 0, k == KC - 1)
                mm.then_inc(scores_ready, 1)

            def product_a(m):
                for k in range(KC):
                    mm = pe.matmul(qT_ps[:, m], wnat[:, 0, k, m * P:(m + 1) * P], wnat[:, 1, k],
                                   start=(k == 0), stop=(k == KC - 1))
                mm.then_inc(a_ready, 1)

            pe.wait_ge(consts_made, 5)
            pe.wait_ge(wqk_in, 16 * 2)
            product_a(0)
            prep_turn(0)
            prep_turn(1)
            product_a(1)
            for m in range(TILES + 2):
                if m == 2:
                    pe.wait_ge(wv_split, 1)
                if m >= 2:
                    prep_v(m - 2)
                if m == 3:
                    pe.wait_ge(a_split, 1)
                    queries(0)
                if 1 < m + 1 < TILES:
                    prep_turn(m + 1)
                if m == 9:
                    pe.wait_ge(v_split, 6)
                if m > 2 and (m - 1) % (CHUNK // P) == 0 or m == TILES + 1:
                    scores(0, 0, (m - 2) // (CHUNK // P))

            def turn_probs(m, t, g):
                if g in (0, HEAD // CHUNK):
                    pe.wait_ge(exp_done, 2 * m + 1 + (g > 0))
                at_least(pe, probs_split, CH * m + g - 1)
                ps = turn_ps[(CH * t + g) % 2]
                for j in range(width(g) // P):
                    at = g * CHUNK + j * P
                    mm = pe.transpose(ps[:, j * P:(j + 1) * P], probs[:, t, at:at + P], ident[:])
                mm.then_inc(probs_turned, 1)

            def values(m, t, g):
                pe.wait_ge(probs_split, CH * m + g + 1)
                if g == 0:
                    at_least(pe, attn_taken, m - 1)
                s = (CH * t + g) % 2
                last = width(g) // P - 1
                for j in range(last + 1):
                    key_tile = g * (CHUNK // P) + j
                    hi, lo = probsT_hi[:, s, j * P:(j + 1) * P], probsT_lo[:, s, j * P:(j + 1) * P]
                    v = v_hi[:, key_tile * VW:(key_tile + 1) * VW]
                    end = g == CH - 1 and j == last
                    pe.matmul(attn_ps[t][:, 0:VW], hi, v, start=(key_tile == 0), stop=False)
                    pe.matmul(attn_ps[t][:, 0:D], hi, v_lo[:, key_tile * VW:key_tile * VW + D], start=False, stop=False)
                    mm = pe.matmul(attn_ps[t][:, 0:VW], lo, v, start=False, stop=end)
                mm.then_inc(values_done, 1)

            def turn_xhat(m, t):
                pe.wait_ge(xhat_ready, m + 1)
                at_least(pe, gates_ready, m)
                for k in range(KC):
                    mm = pe.transpose(rT_ps[:, k], xhat[:, t, k * P:(k + 1) * P], ident[:])
                mm.then_inc(xhat_turned, 1)

            def logits(m):
                pe.wait_ge(router_split, m + 1)
                for k in range(KC):
                    pe.matmul(logits2_ps, rT_hi[:, k], rwT[:, k], start=(k == 0), stop=False)
                    mm = pe.matmul(logits_ps, rT_lo[:, k], rwT[:, k, 0:E], start=False, stop=(k == KC - 1))
                mm.then_inc(logits_ready, 1)

            def ranks(m):
                pe.wait_ge(picks_ready, m + 1)
                pe.matmul(rank_ps, before[:], picked[:], start=True, stop=True)
                pe.matmul(total_ps, ones[:], picked[:], start=True, stop=True).then_inc(ranks_ready, 1)

            def step(n, t, next_block=None, new=AT_PACE, post=True, late=True):
                m, u = n - 1, 1 - t
                for g in range(CH + 2):
                    for chunk in new[g]:
                        scores(n, t, chunk)
                    if next_block is not None and g == 2:
                        queries(next_block)
                    if 1 <= g <= CH:
                        turn_probs(m, u, g - 1)
                    if late and g == 1:
                        ranks(n - 3)
                    if post and g == 4:
                        turn_xhat(n - 2, t)
                    if post and g == 6:
                        logits(n - 2)
                    if g >= 2:
                        values(m, u, g - 2)

            pe.wait_ge(v_split, TILES)
            pe.wait_ge(v_columns_made, 2)
            pe.wait_ge(rw_split, 1)
            step(1, 1, next_block=1, post=False, late=False)
            step(2, 0, late=False)
            with pe.Fori(1, BLOCKS - 1) as b:
                step(2 * b + 1, 1, next_block=b + 1)
                step(2 * b + 2, 0)
            step(TILES - 1, 1, new=AHEAD_OF_PACE)

            def turn_fx(b):
                pe.wait_ge(fx_ready, b + 1)
                at_least(pe, fx_split, b)
                for k in range(KC):
                    for t in range(2):
                        mm = pe.transpose(qT_ps[:, k, t * P:(t + 1) * P], fx[:, t, k * P:(k + 1) * P], ident[:])
                mm.then_inc(fx_turned, 1)

            def hidden(b):
                pe.wait_ge(fx_split, b + 1)
                for p in range(FP):
                    if isinstance(b, int) and b == 0:
                        pe.wait_ge(w1_split, p + 1)
                    at_least(pe, gelu_done, FP * (b - 1) + p + 1)
                    for i in range(2):
                        f = slice((2 * p + i) * P, (2 * p + i + 1) * P)
                        for k in range(KC):
                            mm = split_product(hidden_ps[p][:, i * B:(i + 1) * B],
                                               (w1T[0][:, k, f], w1T[1][:, k, f]),
                                               (qT_hi[:, k], qT_lo[:, k]), k == 0, k == KC - 1)
                    mm.then_inc(hidden_ready, 1)

            def output(b):
                at_least(pe, y_taken, 2 * b)
                for p in range(FP):
                    pe.wait_ge(hidden_split, FP * b + p + 1)
                    if isinstance(b, int) and b == 0:
                        pe.wait_ge(w2_split, p + 1)
                    for i in range(2):
                        f = 2 * p + i
                        for t in range(2):
                            cols = slice(t * P, (t + 1) * P)
                            mm = split_product(y_ps[t][:, 0:D], (hT_hi[:, f, cols], hT_lo[:, f, cols]),
                                               (w2T[0][:, f], w2T[1][:, f]), f == 0, f == FT - 1)
                    mm.then_inc(hidden_used, 1)

            def last_output(b):
                pe.wait_ge(y_taken, 2 * b)
                half = FP // 2
                pairs = [(t, p) for p in range(half) for t in range(2)] + \
                    [(t, p) for t in range(2) for p in range(half, FP)]
                for t, p in pairs:
                    pe.wait_ge(hidden_split, FP * b + p + 1)
                    for f in (2 * p, 2 * p + 1):
                        cols = slice(t * P, (t + 1) * P)
                        mm = split_product(y_ps[t][:, 0:D], (hT_hi[:, f, cols], hT_lo[:, f, cols]),
                                           (w2T[0][:, f], w2T[1][:, f]), f == 0, f == FT - 1)
                    if p == FP - 1:
                        mm.then_inc(hidden_used, half)

            for g in range(CH + 2):
                if g < CH:
                    turn_probs(TILES - 1, 1, g)
                if 1 <= g <= CH:
                    values(TILES - 1, 1, g - 1)
                if g == 1:
                    ranks(TILES - 3)
                if g == 4:
                    turn_xhat(TILES - 2, 0)
                if g == 5:
                    turn_fx(0)
                if g == 6:
                    logits(TILES - 2)
            hidden(0)
            turn_fx(1)
            pe.wait_ge(attn_taken, TILES)
            output(0)
            ranks(TILES - 2)
            hidden(1)
            turn_xhat(TILES - 1, 1)
            turn_fx(2)
            output(1)
            logits(TILES - 1)
            hidden(2)
            turn_fx(3)
            output(2)
            ranks(TILES - 1)
            with pe.Fori(3, BLOCKS - 1) as b:
                hidden(b)
                turn_fx(b + 1)
                output(b)
            hidden(BLOCKS - 1)
            last_output(BLOCKS - 1)

        @block.scalar
        def _(act):
            a = nc.scalar
            act.dma_start(wnat[:, 0], Wq.rearrange("(k p) d -> p k d", p=P)).then_inc(wqk_in, 16)
            act.dma_start(wnat[:, 1], Wk.rearrange("(k p) d -> p k d", p=P)).then_inc(wqk_in, 16)
            act.dma_start(rwnat, router_wT.rearrange("(k p) e -> p k e", p=P)).then_inc(rw_in, 16)

            def copy(dst, src):
                return a.activation(dst, src, ACT.Copy)

            def make_mask(n, t, half):
                act.wait_ge(edges_in, 16 * n)
                at_least(act, scores_taken, CH * (n - 1))
                keys = slice(half * (KEYS // 2), (half + 1) * (KEYS // 2))
                ins = a.activation(no_edge[:, t, keys], edges_sb[:, keys], ACT.Copy, bias=NO_EDGE, scale=-NO_EDGE)
                if half:
                    ins.then_inc(mask_ready, 1)

            def first_mask(g):
                act.wait_ge(edges_in, 16)
                keys = slice(g * CHUNK, g * CHUNK + width(g))
                a.activation(no_edge[:, 0, keys], edges_sb[:, keys], ACT.Copy, bias=NO_EDGE, scale=-NO_EDGE) \
                    .then_inc(first_mask_ready, 1)

            def prep_norm(m):
                i = group_of(m)
                act.wait_ge(norm1_ready, 2 * i + 2)
                at_least(act, xn_turned, m - len(xn_ring) + 1)
                a.activation(xn_ring[m % len(xn_ring)], tokens[:, m * D:(m + 1) * D], ACT.Identity,
                             bias=shift1[:, m:m + 1], scale=rstd1[:, m:m + 1]).then_inc(xn_ready, 1)

            def prep_hi(m):
                act.wait_ge(xn_turned, m + 1)
                copy(xnT_hi[:, :, m * P:(m + 1) * P],
                     prep_ps[m % len(prep_ps)][:, 0:KC * P].rearrange("p (k t) -> p k t", k=KC)) \
                    .then_inc(xn_hi_out, 1)

            def prep_v(m):
                act.wait_ge(v_ready, m + 1)
                copy(v_hi[:, m * VW:m * VW + D], v_ps[m][:, 0:D]).then_inc(v_hi_out, 1)

            def queries_hi(n, h, b):
                act.wait_ge(q_ready, b + 1)
                at_least(act, q_split, n)
                at_least(act, scores_ready, CH * (n - 1))
                copy(qT_hi[:, :, h * P:(h + 1) * P], qT_ps[:, :, h * P:(h + 1) * P]).then_inc(q_hi_out, 1)

            NORM_AHEAD = 3
            prep_norm(0)
            prep_norm(1)
            act.wait_ge(wv_in, 16)
            copy(wvT_hi, wnat[:, 2]).then_inc(wv_hi_out, 1)
            prep_hi(0)
            prep_hi(1)
            prep_norm(2)
            for m in range(TILES + 3):
                if 2 <= m < TILES:
                    prep_hi(m)
                if m + NORM_AHEAD < TILES:
                    prep_norm(m + NORM_AHEAD)
                if m == 1:
                    act.wait_ge(a_ready, KC)
                    copy(a_hi[:], qT_ps).then_inc(a_hi_out, 1)
                if m == 3:
                    act.wait_ge(rw_in, 16)
                    copy(rwT[:, :, 0:E], rwnat).then_inc(rw_hi_out, 1)
                if m >= 3:
                    prep_v(m - 3)
                if m == 3:
                    queries_hi(0, 0, 0)
                    queries_hi(1, 1, 0)
                if m % (CHUNK // P) == 3:
                    first_mask(m // (CHUNK // P))

            def exps(m, t, parts=(0, 1)):
                act.wait_ge(minus_max_ready, m + 1)
                for i in parts:
                    part = probs[:, t, (0, HEAD)[i]:(HEAD, KEYS)[i]]
                    a.activation(part, part, ACT.Exp, bias=minus_max[:, t:t + 1]).then_inc(exp_done, 1)

            def probs_hi(m, t, g):
                act.wait_ge(probs_turned, CH * m + g + 1)
                at_least(act, values_done, CH * m + g - 1)
                s = (CH * t + g) % 2
                copy(probsT_hi[:, s, 0:width(g)], turn_ps[s][:, 0:width(g)]).then_inc(probs_hi_out, 1)

            def router_hi(m):
                act.wait_ge(xhat_turned, m + 1)
                at_least(act, logits_ready, m)
                copy(rT_hi[:], rT_ps).then_inc(router_hi_out, 1)

            def router_exps(m):
                act.wait_ge(best_ready, m + 1)
                at_least(act, gates_ready, m)
                a.activation(router_exp[:], logits_sb[:], ACT.Exp, bias=best[:, 1:2],
                             accum_out=router_sum[:]).then_inc(router_exp_done, 1)

            def step(n, t, next_block=None, post=True, mask=True, last=False):
                exps(n - 1, 1 - t)
                for g in range(CH):
                    probs_hi(n - 1, 1 - t, g)
                    if last and g in LAST_EXPS:
                        exps(n, t, parts=(LAST_EXPS.index(g),))
                    if g == 3 and post:
                        router_hi(n - 2)
                    if g == 2 and next_block is not None:
                        queries_hi(n + 1, 1 - t, next_block)
                    if g in (0, 4) and mask:
                        make_mask(n + 1, 1 - t, half=g // 4)
                    if g == CH - 1 and post:
                        router_exps(n - 2)

            step(1, 1, next_block=1, post=False)
            step(2, 0, next_block=1)
            with act.Fori(1, BLOCKS - 1) as b:
                step(2 * b + 1, 1, next_block=b + 1)
                step(2 * b + 2, 0, next_block=b + 1)
            step(TILES - 1, 1, mask=False, last=True)

            def fx_hi(b):
                act.wait_ge(fx_turned, b + 1)
                at_least(act, hidden_ready, FP * b)
                copy(qT_hi[:], qT_ps).then_inc(fx_hi_out, 1)

            def w2_hi(p):
                act.wait_ge(w2_in, 16)
                copy(w2T[0][:, 2 * p:2 * p + 2], w2nat[:, 2 * p:2 * p + 2]).then_inc(w2_hi_out, 1)

            def w1_hi(p):
                act.wait_ge(w1_in, 16)
                copy(w1T[0][:, :, p * B:(p + 1) * B], w1nat[:, :, p * B:(p + 1) * B]).then_inc(w1_hi_out, 1)

            def gelu(b, p):
                act.wait_ge(hidden_ready, FP * b + p + 1)
                at_least(act, hidden_split, FP * (b - 1) + p + 1)
                for i in range(2):
                    f = 2 * p + i
                    ins = a.activation(hT[:, f], hidden_ps[p][:, i * B:(i + 1) * B], ACT.Gelu, bias=b1_sb[:, f:f + 1])
                ins.then_inc(gelu_done, 1)

            def hidden_hi(b, p):
                act.wait_ge(gelu_done, FP * b + p + 1)
                at_least(act, hidden_used, FP * (b - 1) + p + 1)
                copy(hT_hi[:, 2 * p:2 * p + 2], hT[:, 2 * p:2 * p + 2]).then_inc(hidden_hi_out, 1)

            def ffn(b, more=True):
                for p in range(FP + 1):
                    if p < FP:
                        gelu(b, p)
                    if p > 0:
                        hidden_hi(b, p - 1)
                if more:
                    fx_hi(b + 1)

            act.wait_ge(scores_ready, CH * TILES)
            for g in range(CH):
                probs_hi(TILES - 1, 1, g)
                if g < FP:
                    w2_hi(g)
                if g == 4:
                    router_hi(TILES - 2)
                if g == 5:
                    fx_hi(0)
                if g >= CH - FP:
                    w1_hi(g - (CH - FP))
            router_exps(TILES - 2)
            act.wait_ge(biases_in, 16 * 2)
            ffn(0)
            ffn(1)
            router_hi(TILES - 1)
            ffn(2)
            router_exps(TILES - 1)
            ffn(3)
            with act.Fori(4, BLOCKS - 1) as b:
                ffn(b)
            ffn(BLOCKS - 1, more=False)

        @block.vector
        def _(dve):
            v = nc.vector

            def lo(dst, src, hi):
                return v.tensor_tensor(dst, src, hi, ALU.subtract)

            ones_col = v_hi[:].rearrange("p (t w) -> p t w", t=TILES)[:, :, D:D + 1]
            zero_col = v_hi[:].rearrange("p (t w) -> p t w", t=TILES)[:, :, D + 1:D + 2]
            v.memset(ones_col.bitcast(F32), 1.0).then_inc(v_columns_made, 1)
            v.memset(zero_col.bitcast(F32), 0.0).then_inc(v_columns_made, 1)
            v.memset(queue[:], 0.0).then_inc(gate_seq, 1)
            st = stats[:].rearrange("p (t s) -> p t s", t=TILES)

            def statistics(m):
                if m in [first_tile for first_tile, _ in GROUPS]:
                    dve.wait_ge(x_in[group_of(m)], 16)
                v.bn_stats(st[:, m], tokens[:, m * D:(m + 1) * D]).then_inc(stats_made, 1)

            def normalise(dst, m, mean, rstd):
                return v.tensor_scalar(dst, tokens[:, tile_of(m)], mean[:, ds(m, 1)], rstd[:, ds(m, 1)],
                                       ALU.subtract, ALU.mult)

            def prep_lo(m):
                dve.wait_ge(xn_hi_out, m + 1)
                tile = slice(m * P, (m + 1) * P)
                lo(xnT_lo[:, :, tile], prep_ps[m % len(prep_ps)][:, 0:KC * P].rearrange("p (k t) -> p k t", k=KC),
                   xnT_hi[:, :, tile]).then_inc(xn_split, 1)

            def prep_v(m):
                dve.wait_ge(v_hi_out, m + 1)
                cols = slice(m * VW, m * VW + D)
                lo(v_lo[:, cols], v_ps[m][:, 0:D], v_hi[:, cols]).then_inc(v_split, 1)

            def queries_lo(n, h):
                dve.wait_ge(q_hi_out, n + 1)
                cols = slice(h * P, (h + 1) * P)
                lo(qT_lo[:, :, cols], qT_ps[:, :, cols], qT_hi[:, :, cols]).then_inc(q_split, 1)

            def take_scores(n, t, g):
                if isinstance(n, int) and n < 2:
                    dve.wait_ge(*((second_mask_ready, CH) if n else (first_mask_ready, g + 1)))
                elif g == 0:
                    at_least(dve, probs_turned, CH * (n - 1))
                    dve.wait_ge(mask_ready, n - 1)
                wait_apart(dve, scores_ready, CH * n + g + 1)
                w = width(g)
                keys = slice(g * CHUNK, g * CHUNK + w)
                v.tensor_tensor_reduce(probs[:, t, keys], score_ps[(CH * t + g) % 2][:, 0:w], no_edge[:, t, keys],
                                       1.0, -BIG, ALU.add, ALU.max, chunk_max[:, t, g:g + 1]) \
                    .then_inc(scores_taken, 1)

            STATISTICS_AHEAD = 10
            for m in range(6):
                statistics(m)
            dve.wait_ge(wv_hi_out, 1)
            lo(wvT_lo, wnat[:, 2], wvT_hi).then_inc(wv_split, 1)
            for m in range(6, STATISTICS_AHEAD):
                statistics(m)
            waiting = list(range(STATISTICS_AHEAD, TILES))
            for m in range(TILES + 3):
                if m < TILES:
                    prep_lo(m)
                for _ in range(2 if m == 3 else 1):
                    if waiting:
                        statistics(waiting.pop(0))
                if m == 1:
                    dve.wait_ge(a_hi_out, 1)
                    lo(a_lo[:], qT_ps, a_hi[:]).then_inc(a_split, 1)
                if m == 3:
                    dve.wait_ge(rw_hi_out, 1)
                    lo(rwT[:, :, E:2 * E], rwnat, rwT[:, :, 0:E]).then_inc(rw_split, 1)
                if m >= 3:
                    prep_v(m - 3)
                if m == 3:
                    queries_lo(0, 0)
                    queries_lo(1, 1)
                if m > 5 and m % (CHUNK // P) == 2:
                    take_scores(0, 0, m // (CHUNK // P) - 1)
            take_scores(0, 0, CH - 1)

            def maximum(n, t):
                dve.wait_ge(scores_taken, CH * (n + 1))
                v.tensor_reduce(row_max[:, t:t + 1], chunk_max[:, t], AX.X, ALU.max).then_inc(max_seq, 1)
                dve.wait_ge(max_seq, n + 1)
                v.tensor_scalar(minus_max[:, t:t + 1], row_max[:, t:t + 1], -1.0, None, ALU.mult) \
                    .then_inc(minus_max_ready, 1)
                v.tensor_scalar(has_edge[:, t:t + 1], row_max[:, t:t + 1], NO_EDGE / 2, None, ALU.is_gt)

            def probs_lo(m, t, g):
                dve.wait_ge(probs_hi_out, CH * m + g + 1)
                s = (CH * t + g) % 2
                w = width(g)
                lo(probsT_lo[:, s, 0:w], turn_ps[s][:, 0:w], probsT_hi[:, s, 0:w]).then_inc(probs_split, 1)

            def finish(m, t):
                seq = FINISH_STEPS * m

                def link(ins, k):
                    ins.then_inc(finish_seq, 1)
                    dve.wait_ge(finish_seq, seq + k)

                dve.wait_ge(values_done, CH * (m + 1))
                link(v.reciprocal(inv_sum[:, t:t + 1], attn_ps[t][:, D:D + 1]), 1)
                link(v.tensor_tensor(row_scale[:, t:t + 1], inv_sum[:, t:t + 1], has_edge[:, t:t + 1], ALU.mult), 2)
                v.scalar_tensor_tensor(out=tokens[:, tile_of(m)], in0=attn_ps[t][:, 0:D], scalar=row_scale[:, t:t + 1],
                                       in1=tokens[:, tile_of(m)], op0=ALU.mult, op1=ALU.add).then_inc(attn_taken, 1)
                wait_apart(dve, attn_taken, m + 1)
                link(v.bn_stats(stats2[:], tokens[:, tile_of(m)]), 3)
                dve.sem_inc(waited_apart, 1)
                link(v.bn_aggr(meanvar2[:], stats2[:]), 4)
                at_least(dve, rstd2_ready, m)
                v.tensor_scalar(var_eps[:], meanvar2[:, 1:2], EPS, None, ALU.add).then_inc(var2_ready, 1)
                link(v.tensor_copy(mean2[:, ds(m, 1)], meanvar2[:, 0:1]), 5)

            def second_norm(m, t):
                dve.wait_ge(rstd2_ready, m + 1)
                dve.wait_ge(finish_seq, FINISH_STEPS * (m + 1))
                at_least(dve, xhat_turned, m - 1)
                normalise(xhat[:, t], m, mean2, rstd2).then_inc(xhat_ready, 1)

            def router_lo(m):
                dve.wait_ge(router_hi_out, m + 1)
                lo(rT_lo[:], rT_ps, rT_hi[:]).then_inc(router_split, 1)

            def route_link(m, ins, k):
                ins.then_inc(route_seq, 1)
                dve.wait_ge(route_seq, ROUTE_STEPS * m + k)

            def pick_first(m):
                dve.wait_ge(logits_ready, m + 1)
                at_least(dve, router_exp_done, m)
                both_parts = logits2_ps.rearrange("p (h e) -> p e h", h=2)
                route_link(m, v.tensor_reduce(logits_sb[:], both_parts, AX.X, ALU.add), 1)
                route_link(m, v.tensor_reduce(best[:, 0:1], logits_sb[:], AX.X, ALU.max), 2)
                v.tensor_scalar(best[:, 1:2], best[:, 0:1], -1.0, None, ALU.mult).then_inc(best_ready, 1)

            def pick_rest(m):
                route_link(m, v.scalar_tensor_tensor(out=cand[:], in0=logits_sb[:], scalar=best[:, 0:1], in1=rev[:],
                                                     op0=ALU.is_equal, op1=ALU.mult), 3)
                route_link(m, v.tensor_reduce(best[:, 2:3], cand[:], AX.X, ALU.max), 4)
                route_link(m, v.tensor_scalar(first[:], rev[:], best[:, 2:3], None, ALU.is_equal), 5)
                route_link(m, v.scalar_tensor_tensor(out=rest[:], in0=first[:], scalar=-BIG, in1=logits_sb[:],
                                                     op0=ALU.mult, op1=ALU.add), 6)
                route_link(m, v.tensor_reduce(best[:, 3:4], rest[:], AX.X, ALU.max), 7)
                route_link(m, v.scalar_tensor_tensor(out=cand[:], in0=rest[:], scalar=best[:, 3:4], in1=rev[:],
                                                     op0=ALU.is_equal, op1=ALU.mult), 8)
                route_link(m, v.tensor_reduce(best[:, 4:5], cand[:], AX.X, ALU.max), 9)
                at_least(dve, ranks_ready, m)
                v.scalar_tensor_tensor(out=picked[:], in0=rev[:], scalar=best[:, 4:5], in1=first[:],
                                       op0=ALU.is_equal, op1=ALU.add).then_inc(picks_ready, 1)

            def gate(m):
                seq = 1 + GATE_STEPS * m
                dve.wait_ge(ranks_ready, m + 1)
                dve.wait_ge(router_exp_done, m + 1)
                v.tensor_tensor(rank[:], rank_ps, queue[:], ALU.add).then_inc(gate_seq, 1)
                v.reciprocal(best[:, 5:6], router_sum[:])
                dve.wait_ge(gate_seq, seq + 1)
                v.tensor_tensor(queue[:], total_ps, queue[:], ALU.add)
                v.scalar_tensor_tensor(out=kept[:], in0=rank[:], scalar=float(CAPACITY), in1=picked[:],
                                       op0=ALU.is_lt, op1=ALU.mult).then_inc(gate_seq, 1)
                dve.wait_ge(gate_seq, seq + 2)
                v.tensor_tensor_reduce(cand[:], kept[:], router_exp[:], 1.0, 0.0, ALU.mult, ALU.add,
                                       best[:, 6:7]).then_inc(gate_seq, 1)
                dve.wait_ge(gate_seq, seq + 3)
                v.tensor_tensor(gates[:, ds(m, 1)], best[:, 6:7], best[:, 5:6], ALU.mult).then_inc(gates_ready, 1)

            def step(n, t, next_block=None, new=AT_PACE, post=True, late=True, last=False):
                m, u = n - 1, 1 - t
                for g in range(CH + 1):
                    if g == 2:
                        probs_lo(m, u, 1)
                    for chunk in new[g]:
                        take_scores(n, t, chunk)
                    if g == 1 or g > 2:
                        probs_lo(m, u, g - 1)
                    if CH - 1 in new[g]:
                        maximum(n, t)
                    if post and g == 1:
                        finish(n - 2, t)
                    if late and g == 2:
                        gate(n - 3)
                    if post and g == 3:
                        second_norm(n - 2, t)
                    if post and g == 4:
                        router_lo(n - 2)
                    if g == 5 and next_block is not None:
                        queries_lo(n + 1, u)
                    if post and g == (CH - 1 if last else CH):
                        pick_first(n - 2)
                    if post and g == CH:
                        pick_rest(n - 2)

            maximum(0, 0)
            step(1, 1, next_block=1, post=False, late=False)
            step(2, 0, next_block=1, late=False)
            with dve.Fori(1, BLOCKS - 1) as b:
                step(2 * b + 1, 1, next_block=b + 1)
                step(2 * b + 2, 0, next_block=b + 1)
            step(TILES - 1, 1, new=AHEAD_OF_PACE, last=True)

            def fx_norm(b):
                at_least(dve, fx_turned, b)
                normalise(fx[:, 0], 2 * b, mean2, rstd2)
                normalise(fx[:, 1], 2 * b + 1, mean2, rstd2).then_inc(fx_ready, 1)

            def fx_lo(b):
                dve.wait_ge(fx_hi_out, b + 1)
                lo(qT_lo[:], qT_ps, qT_hi[:]).then_inc(fx_split, 1)

            def hidden_lo(b, p):
                dve.wait_ge(hidden_hi_out, FP * b + p + 1)
                pair = slice(2 * p, 2 * p + 2)
                lo(hT_lo[:, pair], hT[:, pair], hT_hi[:, pair]).then_inc(hidden_split, 1)

            def result(b):
                dve.wait_ge(hidden_used, FP * (b + 1))
                for t in range(2):
                    v.tensor_tensor(y_sb[:, t], y_ps[t][:, 0:D], b2_sb[:], ALU.add).then_inc(y_taken, 1)
                for t in range(2):
                    m = 2 * b + t
                    dve.wait_ge(y_taken, m + 1)
                    v.scalar_tensor_tensor(out=tokens[:, tile_of(m)], in0=y_sb[:, t], scalar=gates[:, ds(m, 1)],
                                           in1=tokens[:, tile_of(m)], op0=ALU.mult, op1=ALU.add) \
                        .then_inc(out_ready, 1)

            def ffn(b):
                fx_norm(b + 1)
                for p in range(FP):
                    hidden_lo(b, p)
                fx_lo(b + 1)
                result(b)

            for g in range(CH):
                probs_lo(TILES - 1, 1, g)
                if g == 0:
                    finish(TILES - 2, 0)
                if g == 1:
                    gate(TILES - 3)
                if g == 2:
                    second_norm(TILES - 2, 0)
                    dve.wait_ge(probs_turned, CH * (TILES - 1))
                    fx_norm(0)
                if g == 4:
                    router_lo(TILES - 2)
                if g == 5:
                    fx_lo(0)
            pick_first(TILES - 2)
            finish(TILES - 1, 1)
            fx_norm(1)
            for p in range(FP):
                hidden_lo(0, p)
            fx_lo(1)
            pick_rest(TILES - 2)
            dve.wait_ge(gates_ready, 2)
            dve.wait_ge(biases_in, 16 * 2)
            result(0)
            gate(TILES - 2)
            second_norm(TILES - 1, 1)
            fx_norm(2)
            for p in range(FP):
                hidden_lo(1, p)
            router_lo(TILES - 1)
            fx_lo(2)
            result(1)
            fx_norm(3)
            for p in range(FP):
                hidden_lo(2, p)
            pick_first(TILES - 1)
            fx_lo(3)
            pick_rest(TILES - 1)
            result(2)
            gate(TILES - 1)
            dve.wait_ge(gates_ready, TILES)
            with dve.Fori(3, BLOCKS - 1) as b:
                ffn(b)
            b = BLOCKS - 1
            for p in range(FP):
                hidden_lo(b, p)
            for t in range(2):
                m = 2 * b + t
                dve.wait_ge(hidden_used, FP * b + (t + 1) * (FP // 2))
                v.tensor_tensor(y_sb[:, t], y_ps[t][:, 0:D], b2_sb[:], ALU.add).then_inc(y_taken, 1)
                dve.wait_ge(y_taken, m + 1)
                v.scalar_tensor_tensor(out=tokens[:, tile_of(m)], in0=y_sb[:, t], scalar=gates[:, m:m + 1],
                                       in1=tokens[:, tile_of(m)], op0=ALU.mult, op1=ALU.add).then_inc(out_ready, 1)


def kernel(**inputs):
    import numpy as _np
    import concourse.bacc as _bacc
    from concourse import mybir as _mybir
    from concourse.bass_utils import run_bass_kernel_spmd as _run

    n, d = inputs["x"].shape
    pad = -n % P
    laid_out = {
        "x": _np.pad(inputs["x"], ((0, pad), (0, 0))),
        "edges": _np.pad(_np.asarray(inputs["adj"]).T, ((0, pad), (0, pad))),
        "wq": inputs["L0_gnn_Wq"],
        "wk": inputs["L0_gnn_Wk"],
        "wvT": _np.asarray(inputs["L0_gnn_Wv"]).T,
        "router_wT": _np.asarray(inputs["L0_ffn_router_w"]).T,
        "w1T": _np.asarray(inputs["L0_ffn_w1"]).T,
        "b1": inputs["L0_ffn_b1"],
        "w2T": _np.asarray(inputs["L0_ffn_w2"]).T,
        "b2": inputs["L0_ffn_b2"],
    }
    nc = _bacc.Bacc("TRN2", target_bir_lowering=False, num_devices=1)
    arrays, args = {}, []
    for name, array in laid_out.items():
        a = _np.ascontiguousarray(array)
        arrays[f"in_{name}"] = a
        args.append(nc.dram_tensor(f"in_{name}", a.shape, _mybir.dt.from_np(a.dtype), kind="ExternalInput").ap())
    args.append(nc.dram_tensor("out", (n + pad, d), _mybir.dt.float32, kind="ExternalOutput").ap())
    build(nc, *args)
    r = _run(nc, [arrays], core_ids=[0])
    return r.results[0]["out"][:n]
```
